# Optimizing a Trainium2 kernel written in Bass

```python
import numpy as np
import jax
import jax.numpy as jnp

def _softmax(x, axis=-1):
    return jax.nn.softmax(x, axis=axis)

def _gelu(x):
    return jax.nn.gelu(x, approximate=True)

def _silu(x):
    return jax.nn.silu(x)

def _sigmoid(x):
    return jax.nn.sigmoid(x)

def _layernorm(x, axis=-1, eps=1e-05):
    m = jnp.mean(x, axis=axis, keepdims=True)
    v = jnp.var(x, axis=axis, keepdims=True)
    return (x - m) / jnp.sqrt(v + eps)

def _scatter_add(tgt, idx, src, axis=0):
    return tgt.at[idx].add(src)

def _segment_sum(src, seg, n):
    return jax.ops.segment_sum(src, seg, n)
kernel_name = 'mk_gnn_preln_d1_gnn_r8_98e71b'

def setup_inputs(seed: int=0):
    np.random.seed(seed)
    _w = jnp.asarray

    def _rec_inputs():
        import jax
        import jax.numpy as jnp
        _gk = jax.random.key(seed)
        x = -0.0005121 + 1.001 * jax.random.normal(jax.random.fold_in(_gk, 1), (12500, 64), jnp.float32)
        _s = jax.random.randint(jax.random.fold_in(_gk, 2), (100000,), 0, 12500, jnp.int32)
        _d = jax.random.randint(jax.random.fold_in(_gk, 3), (100000,), 0, 12500, jnp.int32)
        _loop = jnp.arange(12500, dtype=jnp.int32)
        src = jnp.concatenate([_s, _d, _loop])
        dst = jnp.concatenate([_d, _s, _loop])
        _o = jnp.argsort(dst, stable=True)
        src = src[_o]
        dst = dst[_o]
        edge_weight1 = jax.random.uniform(jax.random.fold_in(_gk, 12), (212500, 1), jnp.float32, 0.0, 0.999999)
        return (x, src, dst, edge_weight1)
    x, src, dst, edge_weight1 = _rec_inputs()

    def _L0_gnn_setup():
        import jax, jax.numpy as jnp
        import numpy as np
        N_NODES = 6250
        N_EDGES = 100000
        NODE_NF = 64
        HIDDEN_NF = 128

        def _linear_params(key, fan_in, fan_out):
            kw, kb = jax.random.split(key)
            bound = 1.0 / np.sqrt(fan_in)
            W = jax.random.uniform(kw, (fan_in, fan_out), minval=-bound, maxval=bound, dtype=jnp.float32)
            b = jax.random.uniform(kb, (fan_out,), minval=-bound, maxval=bound, dtype=jnp.float32)
            return (W, b)
        key = jax.random.key(seed)
        ks = jax.random.split(key, 8)
        h = jax.random.normal(ks[0], (N_NODES, NODE_NF), dtype=jnp.float32)
        row = jax.random.randint(ks[1], (N_EDGES,), 0, N_NODES)
        col = jax.random.randint(ks[2], (N_EDGES,), 0, N_NODES)
        dist = jax.random.uniform(ks[3], (N_EDGES, 1), dtype=jnp.float32)
        eW1, eb1 = _linear_params(ks[4], 2 * NODE_NF + 1, HIDDEN_NF)
        eW2, eb2 = _linear_params(ks[5], HIDDEN_NF, HIDDEN_NF)
        nW1, nb1 = _linear_params(ks[6], HIDDEN_NF + NODE_NF, HIDDEN_NF)
        nW2, nb2 = _linear_params(ks[7], HIDDEN_NF, NODE_NF)
        return {'h': h, 'row': row, 'col': col, 'dist': dist, 'eW1': eW1, 'eb1': eb1, 'eW2': eW2, 'eb2': eb2, 'nW1': nW1, 'nb1': nb1, 'nW2': nW2, 'nb2': nb2}
    _L0_gnn_all = _L0_gnn_setup()
    _L0_gnn_in = {k: v for k, v in _L0_gnn_all.items() if k in ('eW1', 'eb1', 'eW2', 'eb2', 'nW1', 'nb1', 'nW2', 'nb2')}
    del _L0_gnn_all
    return {'x': x, 'src': src, 'dst': dst, 'edge_weight1': edge_weight1, 'L0_gnn_eW1': _L0_gnn_in['eW1'], 'L0_gnn_eb1': _L0_gnn_in['eb1'], 'L0_gnn_eW2': _L0_gnn_in['eW2'], 'L0_gnn_eb2': _L0_gnn_in['eb2'], 'L0_gnn_nW1': _L0_gnn_in['nW1'], 'L0_gnn_nb1': _L0_gnn_in['nb1'], 'L0_gnn_nW2': _L0_gnn_in['nW2'], 'L0_gnn_nb2': _L0_gnn_in['nb2']}

def reference(x, src, dst, edge_weight1, L0_gnn_eW1, L0_gnn_eb1, L0_gnn_eW2, L0_gnn_eb2, L0_gnn_nW1, L0_gnn_nb1, L0_gnn_nW2, L0_gnn_nb2):
    import jax
    import jax.numpy as jnp

    def _L0_gnn_ref(h, row, col, dist, eW1, eb1, eW2, eb2, nW1, nb1, nW2, nb2):
        import jax, jax.numpy as jnp
        import numpy as np
        N_NODES = 6250
        N_EDGES = 100000
        NODE_NF = 64
        HIDDEN_NF = 128

        def _linear_params(key, fan_in, fan_out):
            kw, kb = jax.random.split(key)
            bound = 1.0 / np.sqrt(fan_in)
            W = jax.random.uniform(kw, (fan_in, fan_out), minval=-bound, maxval=bound, dtype=jnp.float32)
            b = jax.random.uniform(kb, (fan_out,), minval=-bound, maxval=bound, dtype=jnp.float32)
            return (W, b)
        edge_in = jnp.concatenate([h[row], h[col], dist], axis=1)
        e = jax.nn.silu(edge_in @ eW1 + eb1)
        e = jax.nn.silu(e @ eW2 + eb2)
        agg = jax.ops.segment_sum(e, row, num_segments=h.shape[0])
        node_in = jnp.concatenate([h, agg], axis=1)
        out = jax.nn.silu(node_in @ nW1 + nb1) @ nW2 + nb2
        return out
    h = jnp.maximum(_layernorm(x, axis=-1), 0.0)
    x = x + _L0_gnn_ref(h, src, dst, edge_weight1, L0_gnn_eW1, L0_gnn_eb1, L0_gnn_eW2, L0_gnn_eb2, L0_gnn_nW1, L0_gnn_nb1, L0_gnn_nW2, L0_gnn_nb2)
    return x

_drawn_inputs = setup_inputs


def setup_inputs(seed=0):
    import zlib

    import numpy as np

    out = dict(_drawn_inputs(seed))
    spreads = {}
    factors = {'edge_weight1': 43.543, 'L0_gnn_eb1': 2.706, 'L0_gnn_nb1': 4.602}
    for name, (base, spread) in spreads.items():
        noise = np.random.default_rng([zlib.crc32(name.encode()), seed]).standard_normal(out[name].shape)
        drawn = base * np.exp(spread * noise) if base else spread * noise
        out[name] = jnp.asarray(drawn.astype(out[name].dtype))
    for name, factor in factors.items():
        out[name] = (out[name] * factor).astype(out[name].dtype)
    return out
```

```python
import concourse.bass as bass
from concourse import mybir
from contextlib import ExitStack

N, NF, HF = 12500, 64, 128
E = 212500
P = 128
NB = (N + P - 1) // P
NPAD = NB * P
LAST = N - (NB - 1) * P
NBIN = NB + 1
C = 1664
LASTC = E - (P - 1) * C
GC = 4
U = 4
NG = 440
NT = NG * U
ROWS = (NG + 1) * U * P
EPS = 1e-5


def ge(eng, sem, val):
    if not isinstance(val, int) or val > 0:
        eng.wait_ge(sem, val)


def gnn(nc, x, src, dst, ew, eW1, eb1, eW2, eb2, nW1, nb1, nW2, nb2, out):
    fp32, bf16, i32 = mybir.dt.float32, mybir.dt.bfloat16, mybir.dt.int32
    ALU, ACT, AX = mybir.AluOpType, mybir.ActivationFunctionType, mybir.AxisListType
    ds = bass.ds

    rec_d = nc.dram_tensor("rec_d", (ROWS, 4), i32).ap()
    q_d = nc.dram_tensor("q_d", (NPAD, HF), fp32).ap()
    hT_d = nc.dram_tensor("hT_d", (NF, NPAD), fp32).ap()

    with ExitStack() as ctx:
        def sb(name, shape, dt):
            return ctx.enter_context(nc.sbuf_tensor(name, shape, dt))

        def sem(name):
            return ctx.enter_context(nc.semaphore(name))

        iof = sb("iof", [P, P], fp32)
        iob = sb("iob", [P, P], bf16)
        pidx = sb("pidx", [P, 1], fp32)
        identf = sb("identf", [P, P], fp32)
        identb = sb("identb", [P, P], bf16)
        ones = sb("ones", [P, P], bf16)
        onef = sb("onef", [1, 1], fp32)
        Lm = sb("Lm", [P, P], bf16)
        zb = sb("zb", [P, GC * NBIN], bf16)
        W1ab = sb("W1ab", [NF, 2, HF], fp32)
        c_bc = sb("c_bc", [P, HF], fp32)
        b2_bc = sb("b2_bc", [P, HF], fp32)
        b2s = sb("b2s", [P, 3, HF], bf16)
        b2r = sb("b2r", [P, HF], fp32)
        msk = sb("msk", [P, 3], fp32)
        B2 = sb("B2", [P, U, HF], bf16)
        W2 = sb("W2", [HF, HF], fp32)
        eb1c = sb("eb1c", [HF, 1], fp32)
        nb1c = sb("nb1c", [HF, 1], fp32)
        nW1a = sb("nW1a", [NF, HF], fp32)
        nW1b = sb("nW1b", [HF, HF], fp32)
        nW2s = sb("nW2s", [HF, NF], fp32)
        nb2_bc = sb("nb2_bc", [P, NF], fp32)
        P3 = sb("P3", [P, NB * 3 * HF], bf16)
        BIG = sb("BIG", [P, NPAD], fp32)
        AGG = BIG
        def part(a, n):
            return BIG[:, a:a + n]
        REC = part(0, 4 * C).bitcast(i32).rearrange("p (c w) -> p c w", w=4)
        SRC = part(4 * C, C).bitcast(i32)
        DST = part(5 * C, C).bitcast(i32)
        IDX = part(6 * C, C).bitcast(i32)
        TWv = P3[:, 0:2 * C].bitcast(fp32)
        BT = sb("BT", [1, NT], i32)
        BK = sb("BK", [P, C], bf16)
        OH = [sb(f"OH{j}", [P, GC, NBIN], bf16) for j in range(2)]
        TT = [sb(f"TT{j}", [P, GC, NBIN], fp32) for j in range(2)]
        BASE = [sb(f"BASE{j}", [P, NBIN], fp32) for j in range(2)]
        cnt = [sb(f"cnt{j}", [P, NB], fp32) for j in range(2)]
        cnti = sb("cnti", [P, NB], i32)
        ccol = sb("ccol", [P, 1], fp32)
        posf = [sb(f"posf{j}", [P, GC], fp32) for j in range(2)]
        posi = sb("posi", [P, 2 * GC], i32)
        qa = sb("qa", [P, 2 * GC], i32)
        qb = sb("qb", [P, 2 * GC], i32)
        CB = 7
        NCH = NB // CB
        XC = [sb(f"XC{j}", [P, CB, NF], fp32) for j in range(2)]
        XM = sb("XM", [P, CB, NF], fp32)
        SQ = sb("SQ", [P, CB, NF], fp32)
        H = [sb(f"H{j}", [P, CB, NF], fp32) for j in range(2)]
        st = sb("st", [P, 4, CB], fp32)
        HT = [sb(f"HT{j}", [NF, CB * P], fp32) for j in range(2)]
        QS = [sb(f"QS{j}", [P, CB, HF], fp32) for j in range(2)]
        RS = [sb(f"RS{j}", [P, HF], fp32) for j in range(2)]
        RB = [sb(f"RB{k}", [P, U, 4], i32) for k in range(4)]
        G = [sb(f"G{k}", [P, HF], fp32) for k in range(4 * U)]
        OHb = [sb(f"OHb{k}", [P, U, P], bf16) for k in range(4)]
        OHf = [sb(f"OHf{k}", [P, U, P], fp32) for k in range(4)]
        OHT = [sb(f"OHT{k}", [P, U * P], bf16) for k in range(2)]
        E1 = [sb(f"E1{k}", [HF, U * P], fp32) for k in range(2)]
        E2 = [sb(f"E2{k}", [P, U * HF], fp32) for k in range(2)]
        INI = OHf[0][:, :, :].rearrange("p a b -> p (a b)").bitcast(i32)[:, 0:504]
        IOT = OHf[1]
        MT = OHb[1]
        FX = [XC[j][:, 0:4, :] for j in range(2)]
        FO = [H[j][:, 0:4, :] for j in range(2)]

        banks = [ctx.enter_context(nc.psum_tensor(f"bk{i}", [P, 512], fp32)) for i in range(8)]

        TPb = [banks[k][:, :].bitcast(bf16)[:, 0:512] for k in range(2)]

        names = ("cst io w ms ed edc o1 f1 hist hs cc ccc m mb bt o2 p2 d2 c2 pos a "
                 "xm sq h t1 ht pq p1 r1 p2c p3 qc fin htd qd ini scat0 scat1 scat2 scat3 "
                 "gt oh st ad tp z1 z2 ap oT of e1 e2 zero var rt hd fz fu fo fd outs one").split()
        s = {n: sem("s_" + n) for n in names}
        s_x = [sem(f"s_x{j}") for j in range(2)]
        s_hq = [sem(f"s_hq{j}") for j in range(2)]
        s_rec = [sem(f"s_rec{k}") for k in range(4)]
        s_g = [sem(f"s_g{k}") for k in range(4 * U)]
        s_fx = [sem(f"s_fx{k}") for k in range(2)]
        s_fh = [sem(f"s_fh{k}") for k in range(2)]
        s_os = [sem(f"s_os{k}") for k in range(2)]
        s_v = sem("s_v")
        NW = 12

        block = ctx.enter_context(nc.Block())
        NI = C // (2 * GC)
        nchunk = [min(4, NB - 4 * q) for q in range((NB + 3) // 4)]
        full = (P - 1) * C

        def stage_out(e, q):
            e.wait_ge(s["ht"], 2 * (q + 1))
            e.dma_start(hT_d[:, q * CB * P:(q + 1) * CB * P], HT[q % 2][:, :]).then_inc(s_hq[q % 2], 16)
            e.wait_ge(s["qc"], CB * (q + 1))
            e.dma_start(q_d[q * CB * P:(q + 1) * CB * P, :].rearrange("(b p) f -> p b f", p=P),
                        QS[q % 2][:, :, :]).then_inc(s_hq[q % 2], 16)

        def store(e, q):
            nb = nchunk[q]
            e.wait_ge(s["fo"], q + 1)
            rows = out[q * 512:min(N, q * 512 + nb * P), :]
            k = rows.shape[0] // P
            e.dma_start(rows[0:k * P, :].rearrange("(b p) f -> p b f", p=P), FO[q % 2][:, 0:k, :])\
             .then_inc(s_os[q % 2], 16)
            if k < nb:
                e.dma_start(rows[k * P:, :], FO[q % 2][0:LAST, k, :]).then_inc(s_os[q % 2], 16)

        @block.sync
        def _(e):
            e.wait_ge(s["ms"], 3)
            for t, a in ((SRC, src), (DST, dst)):
                e.dma_start(t[0:P - 1, :], a[0:full].rearrange("(p c) -> p c", c=C)).then_inc(s["ed"], 16)
                e.dma_start(t[P - 1:P, 0:LASTC], a[full:E].rearrange("(p c) -> p c", c=LASTC)).then_inc(s["ed"], 16)
            e.wait_ge(s["ini"], 1)
            for k in range(14):
                e.dma_start(rec_d.rearrange("(a p r) w -> a p (r w)", a=14, p=P)[k], INI).then_inc(s["zero"], 16)
            for t, a in ((W1ab[:, 0, :], eW1[0:NF, :]), (W1ab[:, 1, :], eW1[NF:2 * NF, :]),
                         (c_bc[:, :], eW1[2 * NF:2 * NF + 1, :].broadcast_to([P, HF])),
                         (b2_bc[:, :], eb2.rearrange("(a n) -> a n", a=1).broadcast_to([P, HF])),
                         (W2[:, :], eW2), (eb1c[:, :], eb1.rearrange("(n a) -> n a", a=1)),
                         (nb1c[:, :], nb1.rearrange("(n a) -> n a", a=1)),
                         (nW1a[:, :], nW1[0:NF, :]), (nW1b[:, :], nW1[NF:NF + HF, :]), (nW2s[:, :], nW2),
                         (nb2_bc[:, :], nb2.rearrange("(a n) -> a n", a=1).broadcast_to([P, NF]))):
                e.dma_start(t, a).then_inc(s["w"], 16)

            def load_x(t, c0, nb, sm):
                rows = x[c0 * P:min(N, (c0 + nb) * P), :]
                k = rows.shape[0] // P
                e.dma_start(t[:, 0:k, :], rows[0:k * P, :].rearrange("(b p) f -> p b f", p=P)).then_inc(sm, 16)
                if k < nb:
                    e.dma_start(t[0:LAST, k, :], rows[k * P:, :]).then_inc(sm, 16)

            for q in range(NCH):
                ge(e, s["xm"], q - 1)
                if q == NCH - 1:
                    e.wait_ge(s["ms"], 4)
                load_x(XC[q % 2], q * CB, CB, s_x[q % 2])
                if q:
                    stage_out(e, q - 1)
            stage_out(e, NCH - 1)
            for k in range(4):
                e.wait_ge(s[f"scat{k}"], 16 * (C // 4))
            rg = rec_d.rearrange("(g p u) w -> p g (u w)", p=P, u=U)

            def load_rec(i, k):
                g = i * 4 + k
                ge(e, s["st"], g - 3)
                ge(e, s["oh"], g - 3)
                e.dma_start(RB[k][:, :, :].rearrange("p u w -> p (u w)"),
                            rg[:, ds(g, 1), :].rearrange("p a w -> p (a w)")).then_inc(s_rec[k], 16)
            for k in range(4):
                load_rec(0, k)
            with e.Fori(1, NG // 4) as i:
                for k in range(4):
                    load_rec(i, k)
            for q, nb in enumerate(nchunk):
                ge(e, s["fo"], q - 1)
                ge(e, s["fz"], q - 1)
                if q == 0:
                    e.wait_ge(s_hq[0], 32 * (NCH // 2))
                    e.wait_ge(s_hq[1], 32 * (NCH // 2))
                    e.wait_ge(s["xm"], NCH)
                    e.wait_ge(s["h"], NCH)
                e.dma_start(HT[q % 2][:, 0:nb * P], hT_d[:, q * 512:q * 512 + nb * P]).then_inc(s_fh[q % 2], 16)
                load_x(FX[q % 2], q * 4, nb, s_fx[q % 2])
                if q:
                    store(e, q - 1)
            store(e, len(nchunk) - 1)
            for j in range(2):
                n = sum(16 * (1 + (4 * q + nchunk[q] == NB)) for q in range(j, len(nchunk), 2))
                e.wait_ge(s_os[j], n)

        @block.gpsimd
        def _(e):
            e.memset(SRC, NB * P).then_inc(s["ms"], 1)
            e.memset(DST, 0).then_inc(s["ms"], 1)
            e.memset(TWv, 0.0).then_inc(s["ms"], 1)
            e.iota(iof[:, :], pattern=[[1, P]], base=0, channel_multiplier=0,
                   allow_small_or_imprecise_dtypes=True).then_inc(s["io"], 1)
            e.iota(pidx[:, :], pattern=[[0, 1]], base=0, channel_multiplier=1,
                   allow_small_or_imprecise_dtypes=True).then_inc(s["io"], 1)
            e.memset(ones[:, :], 1.0).then_inc(s["io"], 1)
            e.memset(zb[:, :], 0.0).then_inc(s["io"], 1)
            e.memset(onef[:, :], 1.0).then_inc(s["io"], 1)
            iv = INI.rearrange("p (r w) -> p r w", w=4)
            e.memset(INI, 0).then_inc(s["cst"], 1)
            e.wait_ge(s["cst"], 1)
            e.memset(iv.bitcast(fp32)[:, :, 0:1], -1.0).then_inc(s["ini"], 1)
            e.iota(IOT[:, :, :].rearrange("p a b -> p (a b)")[:, 0:440], pattern=[[1, 440]], base=0,
                   channel_multiplier=0, allow_small_or_imprecise_dtypes=True).then_inc(s["io"], 1)
            e.wait_ge(s["zero"], 16 * 14)
            for c in range(C):
                if c % (2 * GC) == 0:
                    e.wait_ge(s["pos"], c // (2 * GC) + 1)
                e.indirect_dma_start(rec_d, bass.IndirectOffsetOnAxis(ap=IDX[:, c:c + 1], axis=0),
                                     REC[:, c, :], None).then_inc(s[f"scat{c % 4}"], 16)
            e.wait_ge(s_hq[0], 32 * (NCH // 2))
            e.wait_ge(s_hq[1], 32 * (NCH // 2))

            def gather(i, k):
                g = i * 4 + k
                for u in range(U):
                    if u == 0:
                        ge(e, s["z1"], g - 3)
                        e.wait_ge(s_rec[k], i * 16 + 16)
                        e.sem_inc(s["gt"], 1)
                    e.indirect_dma_start(G[k * U + u][:, :], None, q_d,
                                         bass.IndirectOffsetOnAxis(ap=RB[k][:, u, 1:2], axis=0))\
                     .then_inc(s_g[k * U + u], 16)
            for k in range(4):
                gather(0, k)
            with e.Fori(1, NG // 4) as i:
                for k in range(4):
                    gather(i, k)

        @block.vector
        def _(e):
            own = [0]

            def link(ins):
                own[0] += 1
                ins.then_inc(s_v, 1)
                e.wait_ge(s_v, own[0])

            e.wait_ge(s["io"], 5)
            link(e.tensor_copy(iob[:, :], iof[:, :]))
            e.tensor_scalar(identf[:, :], iof[:, :], pidx[:, :], None, ALU.is_equal)
            e.tensor_scalar(identb[:, :], iof[:, :], pidx[:, :], None, ALU.is_equal)
            link(e.tensor_scalar(Lm[:, :], iof[:, :], pidx[:, :], None, ALU.is_gt))
            e.wait_ge(s["ed"], 64)
            e.wait_ge(s["edc"], 32)
            link(e.tensor_single_scalar(IDX, SRC, 7, op=ALU.arith_shift_right))
            link(e.tensor_copy(BK[:, :], IDX))
            link(e.tensor_single_scalar(IDX, SRC, 127, op=ALU.bitwise_and))
            e.tensor_copy(REC[:, :, 0:1].bitcast(fp32), IDX.rearrange("p (c w) -> p c w", w=1))
            e.tensor_copy(REC[:, :, 1:2], DST.rearrange("p (c w) -> p c w", w=1))
            link(e.tensor_copy(REC[:, :, 2:3].bitcast(fp32), TWv.rearrange("p (c w) -> p c w", w=1)))
            link(e.memset(REC[:, :, 3:4], 0))
            link(e.memset(SQ[:, :, :], 0.0))
            iota_b = iob[:, 0:NBIN].rearrange("p (a w) -> p a w", a=1).broadcast_to([P, GC, NBIN])

            def onehot(j, g):
                bk = BK[:, ds(g * GC, GC)].rearrange("p (c w) -> p c w", w=1).broadcast_to([P, GC, NBIN])
                return e.tensor_tensor(OH[j][:, :, :], iota_b, bk, ALU.is_equal)

            with e.Fori(0, NI) as i:
                for j in range(2):
                    e.wait_ge(s["f1"], i * 2 + (j + 1))
                    onehot(j, i * 2 + j).then_inc(s["o1"], 1)
            e.wait_ge(s["hist"], 1)
            link(e.tensor_reduce(cnt[0][:, :],
                                 banks[0][:, 0:GC * NBIN].rearrange("p (j w) -> p w j", j=GC)[:, 0:NB, :],
                                 axis=AX.X, op=ALU.add))
            link(e.tensor_scalar(cnti[:, :], cnt[0][:, :], float(P - 1), None, ALU.add))
            link(e.tensor_single_scalar(cnti[:, :], cnti[:, :], 7, op=ALU.arith_shift_right))
            link(e.tensor_copy(cnt[0][:, :], cnti[:, :]))
            a, b, d = 0, 1, 1
            while d < NB:
                e.tensor_copy(cnt[b][:, 0:d], cnt[a][:, 0:d])
                link(e.tensor_tensor(cnt[b][:, d:NB], cnt[a][:, d:NB], cnt[a][:, 0:NB - d], ALU.add))
                a, b, d = b, a, 2 * d
            e.memset(BASE[0][:, 0:1], 0.0)
            e.memset(BASE[0][:, NB:NBIN], float(NT * P))
            link(e.tensor_scalar(BASE[0][:, 1:NB], cnt[a][:, 0:NB - 1], float(P), None, ALU.mult))
            e.sem_inc(s["hs"], 1)
            v0 = own[0]
            NV = 15
            with e.Fori(0, NI) as i:
                n = [0]

                def lk(ins):
                    n[0] += 1
                    ins.then_inc(s_v, 1)

                def at(k):
                    e.wait_ge(s_v, i * NV + (v0 + k))

                for j in range(2):
                    e.wait_ge(s["p2"], i * 2 + (j + 1))
                    onehot(j, i * 2 + j).then_inc(s["o2"], 1)
                for j in range(2):
                    g = i * 2 + j
                    e.wait_ge(s["p2"], g + 3)
                    bs = BASE[j][:, :].rearrange("p (a w) -> p a w", a=1).broadcast_to([P, GC, NBIN])
                    ps = banks[1 + j][:, 0:GC * NBIN].rearrange("p (c w) -> p c w", c=GC)
                    lk(e.tensor_tensor(TT[j][:, :, :], ps, bs, ALU.add))
                    e.wait_ge(s["o2"], g + 1)
                    at(n[0])
                    lk(e.tensor_tensor(TT[j][:, :, :], TT[j][:, :, :], OH[j][:, :, :], ALU.mult))
                    lk(e.tensor_tensor(BASE[1 - j][:, :], banks[3 + j][:, 0:NBIN], BASE[j][:, :], ALU.add))
                    at(n[0])
                    e.sem_inc(s["d2"], 1)
                    lk(e.tensor_reduce(posf[j][:, :], TT[j][:, :, :], axis=AX.X, op=ALU.add))
                    at(n[0])
                    lk(e.tensor_copy(posi[:, j * GC:(j + 1) * GC], posf[j][:, :]))
                at(n[0])
                lk(e.tensor_single_scalar(qa[:, :], posi[:, :], 0x7FFFFE00, op=ALU.bitwise_and))
                lk(e.tensor_scalar(qb[:, :], posi[:, :], 127, 2, ALU.bitwise_and, ALU.logical_shift_left))
                at(n[0])
                lk(e.tensor_tensor(qa[:, :], qa[:, :], qb[:, :], ALU.bitwise_or))
                at(n[0])
                lk(e.tensor_scalar(qb[:, :], posi[:, :], 7, 3, ALU.arith_shift_right, ALU.bitwise_and))
                at(n[0])
                lk(e.tensor_tensor(IDX[:, ds(i * (2 * GC), 2 * GC)], qa[:, :], qb[:, :], ALU.bitwise_or))
                at(n[0])
                e.sem_inc(s["pos"], 1)
                assert n[0] == NV
            own[0] += NV * NI
            e.wait_ge(s["cc"], 1)
            link(e.tensor_copy(ccol[0:NB, :], banks[0][0:NB, 0:1]))
            e.wait_ge(s["io"], 6)
            for k in range(4):
                ge(e, s["mb"], k)
                link(e.tensor_scalar(ccol[0:NB, :], ccol[0:NB, :], -440.0 if k else 0.0, None, ALU.add))
                e.tensor_scalar(MT[0:NB, :, :].rearrange("p a b -> p (a b)")[:, 0:440],
                                IOT[0:NB, :, :].rearrange("p a b -> p (a b)")[:, 0:440],
                                ccol[0:NB, :], None, ALU.is_ge).then_inc(s["m"], 1)
                e.wait_ge(s["mb"], k + 1)
                link(e.tensor_scalar(BT[0:1, k * 440:(k + 1) * 440], banks[0][0:1, 0:440],
                                     float(NB - 1), float(HF), ALU.min, ALU.mult))
            e.wait_ge(s["w"], 16 * 11)
            cur = b2_bc
            for q in range(3):
                e.tensor_scalar(msk[:, q:q + 1], pidx[:, :], float(q), None, ALU.is_equal)
                link(e.tensor_copy(b2s[:, q, :], cur[:, :]))
                if q < 2:
                    link(e.tensor_tensor(b2r[:, :], cur[:, :], b2s[:, q, :], ALU.subtract))
                    cur = b2r
            for q in range(3):
                link(e.tensor_scalar(b2s[:, q, :], b2s[:, q, :], msk[:, q:q + 1], None, ALU.mult))
            link(e.tensor_tensor(b2s[:, 0, :], b2s[:, 0, :], b2s[:, 1, :], ALU.add))
            link(e.tensor_tensor(b2s[:, 0, :], b2s[:, 0, :], b2s[:, 2, :], ALU.add))
            link(e.tensor_copy(B2[:, :, :], b2s[:, 0:1, :].broadcast_to([P, U, HF])))
            def bc(t):
                return t.rearrange("p (b f) -> p b f", f=1).broadcast_to([P, CB, NF])

            for q in range(NCH):
                X = XC[q % 2]
                nx = sum(16 * (1 + (r == NCH - 1)) for r in range(q % 2, q + 1, 2))
                e.wait_ge(s_x[q % 2], nx)
                link(e.tensor_reduce(st[:, 0, :], X[:, :, :], axis=AX.X, op=ALU.add))
                link(e.tensor_scalar(st[:, 1, :], st[:, 0, :], 1.0 / NF, None, ALU.mult))
                link(e.tensor_tensor(XM[:, :, :], X[:, :, :], bc(st[:, 1, :]), ALU.subtract))
                e.sem_inc(s["xm"], 1)
                if q == NCH - 3:
                    e.memset(X[:, CB - 1, :], 0.0).then_inc(s["ms"], 1)
                link(e.tensor_tensor(SQ[:, :, :], XM[:, :, :], XM[:, :, :], ALU.mult))
                link(e.tensor_reduce(st[:, 2, :], SQ[:, :, :], axis=AX.X, op=ALU.add))
                e.tensor_scalar(st[:, 2, :], st[:, 2, :], 1.0 / NF, EPS, ALU.mult, ALU.add).then_inc(s["var"], 1)
                e.wait_ge(s["rt"], q + 1)
                link(e.reciprocal(st[:, 3, :], st[:, 3, :]))
                link(e.tensor_tensor(XM[:, :, :], XM[:, :, :], bc(st[:, 3, :]), ALU.mult))
                ge(e, s["t1"], q - 1)
                e.tensor_scalar(H[q % 2][:, :, :], XM[:, :, :], 0.0, None, ALU.max).then_inc(s["h"], 1)
                for b in range(CB):
                    B = q * CB + b
                    e.wait_ge(s["qc"], B + 1)
                    o = 3 * HF * B
                    pq = banks[4 + B % 2]
                    e.tensor_tensor(RS[B % 2][:, :], pq[:, 0:HF], P3[:, o:o + HF], ALU.subtract).then_inc(s["r1"], 1)
                    e.wait_ge(s["p2c"], B + 1)
                    e.tensor_tensor(P3[:, o + 2 * HF:o + 3 * HF], RS[B % 2][:, :],
                                    P3[:, o + HF:o + 2 * HF], ALU.subtract).then_inc(s["p3"], 1)
            for k in range(4):
                e.wait_ge(s[f"scat{k}"], 16 * (C // 4))
            e.memset(AGG[:, :], 0.0).then_inc(s["ad"], 1)

            def build(i, k):
                g = i * 4 + k
                e.wait_ge(s_rec[k], i * 16 + 16)
                ge(e, s["tp"], g - 3)
                ge(e, s["of"], g - 3)
                for u in range(U):
                    ins = e.tensor_scalar(OHb[k][:, u, :], iob[:, :], RB[k][:, u, 0:1].bitcast(fp32),
                                          None, ALU.is_equal)
                ins.then_inc(s["oh"], 1)
                for u in range(U):
                    e.wait_ge(s_g[k * U + u], i * 16 + 16)
                    ins = e.scalar_tensor_tensor(out=G[k * U + u][:, :], in0=c_bc[:, :],
                                                 scalar=RB[k][:, u, 2:3].bitcast(fp32),
                                                 in1=G[k * U + u][:, :], op0=ALU.mult, op1=ALU.add)
                ins.then_inc(s["st"], 1)

            def add(g, k):
                e.wait_ge(s["ap"], g + 1)
                for u in range(U):
                    v = e.value_load(BT[0:1, ds(g * U + u, 1)], min_val=0, max_val=(NB - 1) * P)
                    e.wait_ge(s["ad"], g * U + (u + 1))
                    e.tensor_tensor(AGG[:, ds(v, P)], banks[6 + k % 2][:, u * P:(u + 1) * P],
                                    AGG[:, ds(v, P)], ALU.add).then_inc(s["ad"], 1)

            for k in range(4):
                build(0, k)
                if k >= 2:
                    add(k - 2, k - 2)
            with e.Fori(1, NG // 4) as i:
                for k in range(4):
                    build(i, k)
                    add(i * 4 + (k - 2), k % 4)
            for g in (NG - 2, NG - 1):
                add(g, g % 4)
            for q, nb in enumerate(nchunk):
                nx = sum(16 * (1 + (4 * r + nchunk[r] == NB)) for r in range(q % 2, q + 1, 2))
                e.wait_ge(s_fx[q % 2], nx)
                if q >= 2:
                    e.wait_ge(s_os[q % 2], 16 * (q // 2))
                nbb = nb2_bc[:, :].rearrange("p (a f) -> p a f", a=1).broadcast_to([P, nb, NF])
                link(e.tensor_tensor(XM[:, 0:nb, :], FX[q % 2][:, 0:nb, :], nbb, ALU.add))
                e.wait_ge(s["fu"], q + 1)
                e.tensor_tensor(FO[q % 2][:, 0:nb, :],
                                banks[2 + q % 2][:, 0:nb * NF].rearrange("p (b f) -> p b f", f=NF),
                                XM[:, 0:nb, :], ALU.add).then_inc(s["fo"], 1)
                link(e.memset(st[:, 0, 0:1], 0.0))

        @block.tensor
        def _(e):
            e.wait_ge(s["io"], 5)
            hp = banks[0][:, 0:GC * NBIN]
            e.matmul(hp, ones[:, :], zb[:, :], start=True, stop=False).then_inc(s["f1"], 2)
            with e.Fori(0, NI) as i:
                for j in range(2):
                    e.wait_ge(s["o1"], i * 2 + (j + 1))
                    e.matmul(hp, ones[:, :], OH[j][:, :, :].rearrange("p a b -> p (a b)"),
                             start=False, stop=False).then_inc(s["f1"], 1)
            e.matmul(hp, ones[:, :], zb[:, :], start=False, stop=True).then_inc(s["hist"], 1)
            e.sem_inc(s["p2"], 2)
            e.sem_inc(s["d2"], 2)
            W = NBIN
            with e.Fori(0, NI) as i:
                for j in range(2):
                    oh = OH[j][:, :, :].rearrange("p a b -> p (a b)")
                    e.wait_ge(s["o2"], i * 2 + (j + 1))
                    e.wait_ge(s["d2"], i * 2 + (j + 1))
                    ps, tot = banks[1 + j], banks[3 + j]
                    for c in range(GC):
                        e.matmul(tot[:, 0:W], ones[:, :], oh[:, c * W:(c + 1) * W], start=(c == 0), stop=(c == GC - 1))
                    e.matmul(ps[:, 0:GC * W], Lm[:, :], oh, start=True, stop=False)
                    for c in range(1, GC):
                        last = e.matmul(ps[:, c * W:GC * W], ones[:, :], oh[:, 0:(GC - c) * W],
                                        start=False, stop=(c == GC - 1))
                    last.then_inc(s["p2"], 1)
            e.wait_ge(s["hs"], 1)
            e.matmul(banks[0][0:NB, 0:1], cnt[1][0:1, :], onef[:, :], start=True, stop=True).then_inc(s["cc"], 1)
            for k in range(4):
                e.wait_ge(s["m"], k + 1)
                e.matmul(banks[0][0:1, 0:440], ones[0:NB, 0:1],
                         MT[0:NB, :, :].rearrange("p a b -> p (a b)")[:, 0:440],
                         start=True, stop=True).then_inc(s["mb"], 1)
            e.wait_ge(s["w"], 16 * 11)
            for q in range(NCH):
                e.wait_ge(s["h"], q + 1)
                for hb in range(2):
                    ge(e, s["ht"], 2 * q - 1 + hb)
                    bs = range(4 * hb, min(CB, 4 * hb + 4))
                    for b in bs:
                        last = e.matmul(banks[6 + hb][0:NF, (b - 4 * hb) * P:(b - 4 * hb + 1) * P],
                                        H[q % 2][:, b, :], identf[:, :], start=True, stop=True)
                    last.then_inc(s["t1"] if hb else s["hd"], 1)
                e.wait_ge(s["ht"], 2 * (q + 1))
                for b in range(CB):
                    B = q * CB + b
                    ge(e, s["r1"], B - 1)
                    ge(e, s["qc"], B - 1)
                    e.matmul(banks[4 + B % 2][:, 0:2 * HF], HT[q % 2][:, b * P:(b + 1) * P],
                             W1ab[:, :, :].rearrange("p a b -> p (a b)"), start=True, stop=True).then_inc(s["pq"], 1)

            def mA(g, k):
                e.wait_ge(s["oh"], g + 1)
                ge(e, s["oT"], g - 1)
                tp = TPb[k % 2]
                for u in range(U):
                    last = e.transpose(tp[:, u * P:(u + 1) * P], OHb[k][:, u, :], identb[:, :])
                last.then_inc(s["tp"], 1)

            def mB(g, k):
                e.wait_ge(s["oT"], g + 1)
                e.wait_ge(s["st"], g + 1)
                ge(e, s["e1"], g - 1)
                for u in range(U):
                    z = banks[2 + k % 2][:, u * P:(u + 1) * P]
                    v = e.value_load(BT[0:1, ds(g * U + u, 1)], min_val=0, max_val=(NB - 1) * P)
                    e.matmul(z, G[k * U + u][:, :], identf[:, :], start=True, stop=False)
                    for q in range(3):
                        last = e.matmul(z, P3[:, ds(v * 3 + q * HF, HF)], OHT[k % 2][:, u * P:(u + 1) * P],
                                        start=False, stop=(q == 2))
                last.then_inc(s["z1"], 1)

            def mC(g, k):
                e.wait_ge(s["e1"], g + 1)
                ge(e, s["e2"], g - 1)
                z = banks[4 + k % 2]
                e.matmul(z[:, :], ones[:, :], B2[:, :, :].rearrange("p a b -> p (a b)"), start=True, stop=False)
                for u in range(U):
                    last = e.matmul(z[:, u * HF:(u + 1) * HF], E1[k % 2][:, u * P:(u + 1) * P], W2[:, :],
                                    start=False, stop=(u == U - 1))
                last.then_inc(s["z2"], 1)

            def mD(g, k):
                e.wait_ge(s["e2"], g + 1)
                e.wait_ge(s["of"], g + 1)
                ge(e, s["ad"], (g - 1) * U + 1)
                for u in range(U):
                    last = e.matmul(banks[6 + k % 2][:, u * P:(u + 1) * P], E2[k % 2][:, u * HF:(u + 1) * HF],
                                    OHf[k][:, u, :], start=True, stop=True)
                last.then_inc(s["ap"], 1)

            e.wait_ge(s["p3"], NB)
            e.wait_ge(s["qc"], NB)
            for k in range(4):
                mA(k, k)
                if k >= 2:
                    mD(k - 2, k - 2)
                if k >= 1:
                    mC(k - 1, k - 1)
                mB(k, k)
            with e.Fori(1, NG // 4) as i:
                for k in range(4):
                    g = i * 4 + k
                    mA(g, k)
                    mD(i * 4 + (k - 2), (k - 2) % 4)
                    mC(i * 4 + (k - 1), (k - 1) % 4)
                    mB(g, k)
            mD(NG - 2, (NG - 2) % 4)
            mC(NG - 1, (NG - 1) % 4)
            mD(NG - 1, (NG - 1) % 4)
            e.wait_ge(s["ad"], NT + 1)
            for q in range(len(nchunk) + 1):
                if q < len(nchunk):
                    nb = nchunk[q]
                    e.wait_ge(s_fh[q % 2], 16 * (q // 2 + 1))
                    ge(e, s["fd"], q - 1)
                    z = banks[q % 2][:, 0:nb * P]
                    e.matmul(z, nW1b[:, :], AGG[:, q * 512:q * 512 + nb * P], start=True, stop=False)
                    e.matmul(z, nW1a[:, :], HT[q % 2][:, 0:nb * P], start=False, stop=True).then_inc(s["fz"], 1)
                if q:
                    r = q - 1
                    e.wait_ge(s["fd"], r + 1)
                    ge(e, s["fo"], r - 1)
                    for b in range(nchunk[r]):
                        last = e.matmul(banks[2 + r % 2][:, b * NF:(b + 1) * NF], E1[r % 2][:, b * P:(b + 1) * P],
                                        nW2s[:, :], start=True, stop=True)
                    last.then_inc(s["fu"], 1)

        @block.scalar
        def _(e):
            e.wait_ge(s["ms"], 3)
            ewf = ew.rearrange("n a -> (n a)")
            e.dma_start(TWv[0:P - 1, :], ewf[0:full].rearrange("(p c) -> p c", c=C)).then_inc(s["edc"], 16)
            e.dma_start(TWv[P - 1:P, 0:LASTC], ewf[full:E].rearrange("(p c) -> p c", c=LASTC)).then_inc(s["edc"], 16)
            for q in range(NCH):
                e.wait_ge(s["var"], q + 1)
                e.activation(st[:, 3, :], st[:, 2, :], ACT.Sqrt).then_inc(s["rt"], 1)
                if q >= 2:
                    e.wait_ge(s_hq[q % 2], 32 * (q // 2))
                for hb in range(2):
                    e.wait_ge(s["t1"] if hb else s["hd"], q + 1)
                    n = (4 - hb) * P
                    e.activation(HT[q % 2][:, hb * 512:hb * 512 + n], banks[6 + hb][0:NF, 0:n],
                                 ACT.Copy).then_inc(s["ht"], 1)
                for b in range(CB):
                    B = q * CB + b
                    o = 3 * HF * B
                    e.wait_ge(s["pq"], B + 1)
                    pq = banks[4 + B % 2]
                    e.activation(P3[:, o:o + HF], pq[:, 0:HF], ACT.Copy).then_inc(s["p1"], 1)
                    e.activation(QS[q % 2][:, b, :], pq[:, HF:2 * HF], ACT.Copy).then_inc(s["qc"], 1)
                    e.wait_ge(s["r1"], B + 1)
                    e.activation(P3[:, o + HF:o + 2 * HF], RS[B % 2][:, :], ACT.Copy).then_inc(s["p2c"], 1)

            def tcopy(g, k):
                e.wait_ge(s["tp"], g + 1)
                ge(e, s["z1"], g - 1)
                e.activation(OHT[k % 2][:, :], TPb[k % 2], ACT.Copy).then_inc(s["oT"], 1)
                ge(e, s["ap"], g - 3)
                e.activation(OHf[k][:, :, :], OHb[k][:, :, :], ACT.Copy).then_inc(s["of"], 1)

            def silu1(g, k):
                e.wait_ge(s["z1"], g + 1)
                ge(e, s["z2"], g - 1)
                e.activation(E1[k % 2][:, :], banks[2 + k % 2][:, :], ACT.Silu, bias=eb1c[:, :]).then_inc(s["e1"], 1)

            def silu2(g, k):
                e.wait_ge(s["z2"], g + 1)
                ge(e, s["ap"], g - 1)
                e.activation(E2[k % 2][:, :], banks[4 + k % 2][:, :], ACT.Silu).then_inc(s["e2"], 1)

            e.wait_ge(s["w"], 16 * 11)
            for k in range(4):
                tcopy(k, k)
                if k:
                    silu2(k - 1, k - 1)
                silu1(k, k)
            with e.Fori(1, NG // 4) as i:
                for k in range(4):
                    g = i * 4 + k
                    tcopy(g, k)
                    silu2(i * 4 + (k - 1), (k - 1) % 4)
                    silu1(g, k)
            silu2(NG - 1, (NG - 1) % 4)
            for q, nb in enumerate(nchunk):
                e.wait_ge(s["fz"], q + 1)
                ge(e, s["fu"], q - 1)
                e.activation(E1[q % 2][:, 0:nb * P], banks[q % 2][:, 0:nb * P], ACT.Silu, bias=nb1c[:, :])\
                 .then_inc(s["fd"], 1)


_INS = ["x", "src", "dst", "edge_weight1", "L0_gnn_eW1", "L0_gnn_eb1", "L0_gnn_eW2", "L0_gnn_eb2",
        "L0_gnn_nW1", "L0_gnn_nb1", "L0_gnn_nW2", "L0_gnn_nb2"]


def kernel(**inputs):
    import numpy as _np
    import concourse.bacc as _bacc
    from concourse import mybir as _mybir
    from concourse.bass_utils import run_bass_kernel_spmd as _run

    nc = _bacc.Bacc("TRN2", target_bir_lowering=False, num_devices=1)
    arrays, args = {}, []
    for name in _INS:
        a = _np.ascontiguousarray(inputs[name])
        arrays[f"in_{name}"] = a
        args.append(nc.dram_tensor(f"in_{name}", a.shape, _mybir.dt.from_np(a.dtype), kind="ExternalInput").ap())
    out = nc.dram_tensor("out_0", (N, NF), _mybir.dt.float32, kind="ExternalOutput").ap()
    gnn(nc, *args, out)
    return _run(nc, [arrays], core_ids=[0]).results[0]["out_0"]
```

```python
import concourse.bass as bass
from concourse import mybir
from contextlib import ExitStack

N, NF, HF = 12500, 64, 128
E = 212500
P = 128
NB = (N + P - 1) // P
NPAD = NB * P
LAST = N - (NB - 1) * P
NBIN = NB + 1
C = 1664
LASTC = E - (P - 1) * C
GC = 4
U = 4
NG = 440
NT = NG * U
ROWS = (NG + 1) * U * P
EPS = 1e-5


def ge(eng, sem, val):
    if not isinstance(val, int) or val > 0:
        eng.wait_ge(sem, val)


def gnn(nc, x, src, dst, ew, eW1, eb1, eW2, eb2, nW1, nb1, nW2, nb2, out):
    fp32, bf16, i32 = mybir.dt.float32, mybir.dt.bfloat16, mybir.dt.int32
    ALU, ACT, AX = mybir.AluOpType, mybir.ActivationFunctionType, mybir.AxisListType
    ds = bass.ds

    rec_d = nc.dram_tensor("rec_d", (ROWS, 4), i32).ap()
    q_d = nc.dram_tensor("q_d", (NPAD, HF), fp32).ap()
    hT_d = nc.dram_tensor("hT_d", (NF, NPAD), fp32).ap()

    with ExitStack() as ctx:
        def sb(name, shape, dt):
            return ctx.enter_context(nc.sbuf_tensor(name, shape, dt))

        def sem(name):
            return ctx.enter_context(nc.semaphore(name))

        iof = sb("iof", [P, P], fp32)
        iob = sb("iob", [P, P], bf16)
        pidx = sb("pidx", [P, 1], fp32)
        identf = sb("identf", [P, P], fp32)
        identb = sb("identb", [P, P], bf16)
        ones = sb("ones", [P, P], bf16)
        onef = sb("onef", [1, 1], fp32)
        Lm = sb("Lm", [P, P], bf16)
        onesf = sb("onesf", [P, P], fp32)
        hp = sb("hp", [P, 2], fp32)
        hpi = sb("hpi", [P, 2], i32)
        W1ab = sb("W1ab", [NF, 2, HF], fp32)
        c_bc = sb("c_bc", [P, HF], fp32)
        b2_bc = sb("b2_bc", [P, HF], fp32)
        b2s = sb("b2s", [P, 3, HF], bf16)
        b2r = sb("b2r", [P, HF], fp32)
        msk = sb("msk", [P, 3], fp32)
        B2 = sb("B2", [P, U, HF], bf16)
        W2 = sb("W2", [HF, HF], fp32)
        eb1c = sb("eb1c", [HF, 1], fp32)
        nb1c = sb("nb1c", [HF, 1], fp32)
        nW1a = sb("nW1a", [NF, HF], fp32)
        nW1b = sb("nW1b", [HF, HF], fp32)
        nW2s = sb("nW2s", [HF, NF], fp32)
        nb2_bc = sb("nb2_bc", [P, NF], fp32)
        P3all = sb("P3", [P, 3 * NPAD], bf16)
        P3 = [P3all[:, q * NPAD:(q + 1) * NPAD] for q in range(3)]
        XA = P3all[:, 0:2 * NB * NF].bitcast(fp32).rearrange("p (b f) -> p b f", f=NF)
        HA = P3all[0:NF, 2 * NB * NF:2 * NB * NF + 2 * NPAD].bitcast(fp32)
        BIG = sb("BIG", [P, NPAD], fp32)
        AGG = BIG
        def part(a, n):
            return BIG[:, a:a + n]
        REC = part(0, 4 * C).bitcast(i32).rearrange("p (c w) -> p c w", w=4)
        SRC = part(4 * C, C).bitcast(i32)
        DST = part(5 * C, C).bitcast(i32)
        IDX = part(6 * C, C).bitcast(i32)
        TWv = P3all[:, 0:2 * C].bitcast(fp32)
        CG = 64
        HI, LO = (P3all[:, a * C:(a + 1) * C] for a in (2, 3))
        o1 = 4 * C
        OA = [P3all[:, o1 + j * CG * 8:o1 + (j + 1) * CG * 8].rearrange("p (c h) -> p c h", h=8) for j in range(2)]
        o1 += 2 * CG * 8
        OB = [P3all[:, o1 + j * CG * 16:o1 + (j + 1) * CG * 16].rearrange("p (c l) -> p c l", l=16) for j in range(2)]
        o1 += 2 * CG * 16
        M1 = P3all[:, o1:o1 + 512].bitcast(fp32).rearrange("p (j l) -> p j l", l=16)
        MK = P3all[:, o1 + 512:o1 + 1024].bitcast(fp32).rearrange("p (j l) -> p j l", l=16)
        RR = P3all[:, o1 + 1024:o1 + 1056].bitcast(fp32)
        BT = sb("BT", [1, NT], i32)
        BK = sb("BK", [P, C + 2 * GC], bf16)
        OH = [sb(f"OH{j}", [P, GC, NBIN], bf16) for j in range(2)]
        TT = [sb(f"TT{j}", [P, GC, NBIN], fp32) for j in range(2)]
        BASE = [sb(f"BASE{j}", [P, NBIN], fp32) for j in range(2)]
        cnt = [sb(f"cnt{j}", [P, NB], fp32) for j in range(2)]
        cnti = sb("cnti", [P, NB], i32)
        ccol = sb("ccol", [P, 1], fp32)
        posf = [sb(f"posf{j}", [P, GC], fp32) for j in range(2)]
        posi = sb("posi", [P, 2 * GC], i32)
        qa = sb("qa", [P, 2 * GC], i32)
        qb = sb("qb", [P, 2 * GC], i32)
        CB = 7
        NCH = NB // CB
        XC = [sb(f"XC{j}", [P, CB, NF], fp32) for j in range(2)]
        XM = sb("XM", [P, CB, NF], fp32)
        SQ = sb("SQ", [P, CB, NF], fp32)
        H = [sb(f"H{j}", [P, CB, NF], fp32) for j in range(2)]
        st = sb("st", [P, 4, CB], fp32)
        HT = [sb(f"HT{j}", [NF, CB * P], fp32) for j in range(2)]
        QS = [sb(f"QS{j}", [P, CB, HF], fp32) for j in range(2)]
        RS = [sb(f"RS{j}", [P, HF], fp32) for j in range(2)]
        RB = [sb(f"RB{k}", [P, U, 4], i32) for k in range(4)]
        G = [sb(f"G{k}", [P, HF], fp32) for k in range(4 * U)]
        OHb = [sb(f"OHb{k}", [P, U, P], bf16) for k in range(4)]
        OHf = [sb(f"OHf{k}", [P, U, P], fp32) for k in range(4)]
        OHT = [sb(f"OHT{k}", [P, U * P], bf16) for k in range(2)]
        E1 = [sb(f"E1{k}", [HF, U * P], fp32) for k in range(2)]
        E2 = [sb(f"E2{k}", [P, U * HF], fp32) for k in range(2)]
        INI = OHf[0][:, :, :].rearrange("p a b -> p (a b)").bitcast(i32)[:, 0:504]
        IOT = OHf[1]
        MT = OHb[1]

        banks = [ctx.enter_context(nc.psum_tensor(f"bk{i}", [P, 512], fp32)) for i in range(8)]

        TPb = [banks[k][:, :].bitcast(bf16)[:, 0:512] for k in range(2)]

        names = ("rr hc fb cst io w ms ed edc o1 f1 hist hs cc ccc m mb bt o2 p2 d2 c2 pos a "
                 "xm sq h t1 ht pq p1 r1 p2c p3 qc fin htd qd ini scat0 scat1 scat2 scat3 "
                 "gt oh st ad tp z1 z2 ap oT of e1 e2 zero var rt hd fz fu fo fd outs one").split()
        s = {n: sem("s_" + n) for n in names}
        s_x = [sem(f"s_x{j}") for j in range(2)]
        s_hq = [sem(f"s_hq{j}") for j in range(2)]
        s_rec = [sem(f"s_rec{k}") for k in range(4)]
        s_g = [sem(f"s_g{k}") for k in range(4 * U)]
        QB = 12
        NQ = (NB + QB - 1) // QB
        s_fx = [sem(f"s_fx{k}") for k in range(NQ)]
        s_v = sem("s_v")
        NW = 12

        def blocks(g, engine):
            return nc.values_load_multi_w_load_instructions(
                BT[0:1, ds(g * U, U)], engines=[engine], min_val=0, max_val=(NB - 1) * P,
                skip_runtime_bounds_check_because="BT is clipped to them when it is made")[1]

        block = ctx.enter_context(nc.Block())
        NI = C // (2 * GC)
        nchunk = [min(4, NB - 4 * q) for q in range((NB + 3) // 4)]
        full = (P - 1) * C

        def stage_out(e, q):
            e.wait_ge(s["ht"], 2 * (q + 1))
            e.dma_start(hT_d[:, q * CB * P:(q + 1) * CB * P], HT[q % 2][:, :]).then_inc(s_hq[q % 2], 16)
            e.wait_ge(s["qc"], CB * (q + 1))
            e.dma_start(q_d[q * CB * P:(q + 1) * CB * P, :].rearrange("(b p) f -> p b f", p=P),
                        QS[q % 2][:, :, :]).then_inc(s_hq[q % 2], 16)

        def store(e, q):
            a, b = q * QB, min(NB, (q + 1) * QB)
            e.wait_ge(s["fo"], min(len(nchunk), (b + 3) // 4))
            rows = out[a * P:min(N, b * P), :]
            k = rows.shape[0] // P
            e.dma_start(rows[0:k * P, :].rearrange("(b p) f -> p b f", p=P), XA[:, a:a + k, :])\
             .then_inc(s["outs"], 16)
            if k < b - a:
                e.dma_start(rows[k * P:, :], XA[0:LAST, a + k, :]).then_inc(s["outs"], 16)

        @block.sync
        def _(e):
            e.wait_ge(s["ms"], 3)
            for t, a in ((SRC, src), (DST, dst)):
                e.dma_start(t[0:P - 1, :], a[0:full].rearrange("(p c) -> p c", c=C)).then_inc(s["ed"], 16)
                e.dma_start(t[P - 1:P, 0:LASTC], a[full:E].rearrange("(p c) -> p c", c=LASTC)).then_inc(s["ed"], 16)
            e.wait_ge(s["ini"], 1)
            for k in range(14):
                e.dma_start(rec_d.rearrange("(a p r) w -> a p (r w)", a=14, p=P)[k], INI).then_inc(s["zero"], 16)
            for t, a in ((W1ab[:, 0, :], eW1[0:NF, :]), (W1ab[:, 1, :], eW1[NF:2 * NF, :]),
                         (c_bc[:, :], eW1[2 * NF:2 * NF + 1, :].broadcast_to([P, HF])),
                         (b2_bc[:, :], eb2.rearrange("(a n) -> a n", a=1).broadcast_to([P, HF])),
                         (W2[:, :], eW2), (eb1c[:, :], eb1.rearrange("(n a) -> n a", a=1)),
                         (nb1c[:, :], nb1.rearrange("(n a) -> n a", a=1)),
                         (nW1a[:, :], nW1[0:NF, :]), (nW1b[:, :], nW1[NF:NF + HF, :]), (nW2s[:, :], nW2),
                         (nb2_bc[:, :], nb2.rearrange("(a n) -> a n", a=1).broadcast_to([P, NF]))):
                e.dma_start(t, a).then_inc(s["w"], 16)

            def load_x(t, c0, nb, sm):
                rows = x[c0 * P:min(N, (c0 + nb) * P), :]
                k = rows.shape[0] // P
                e.dma_start(t[:, 0:k, :], rows[0:k * P, :].rearrange("(b p) f -> p b f", p=P)).then_inc(sm, 16)
                if k < nb:
                    e.dma_start(t[0:LAST, k, :], rows[k * P:, :]).then_inc(sm, 16)

            for q in range(NCH):
                ge(e, s["xm"], q - 1)
                if q == NCH - 1:
                    e.wait_ge(s["ms"], 4)
                load_x(XC[q % 2], q * CB, CB, s_x[q % 2])
                if q:
                    stage_out(e, q - 1)
            stage_out(e, NCH - 1)
            for k in range(4):
                e.wait_ge(s[f"scat{k}"], 16 * (C // 4))
            rg = rec_d.rearrange("(g p u) w -> p g (u w)", p=P, u=U)

            def load_rec(i, k):
                g = i * 4 + k
                ge(e, s["st"], g - 3)
                ge(e, s["oh"], g - 3)
                e.dma_start(RB[k][:, :, :].rearrange("p u w -> p (u w)"),
                            rg[:, ds(g, 1), :].rearrange("p a w -> p (a w)")).then_inc(s_rec[k], 16)
            for k in range(4):
                load_rec(0, k)
            with e.Fori(1, NG // 4) as i:
                for k in range(4):
                    load_rec(i, k)
            e.wait_ge(s["z1"], NG)
            for j in range(2):
                e.wait_ge(s_hq[j], 32 * (NCH // 2))
            for q in range(NQ):
                a, b = q * QB, min(NB, (q + 1) * QB)
                e.dma_start(HA[:, a * P:b * P], hT_d[:, a * P:b * P]).then_inc(s_fx[q], 16)
                load_x(XA[:, a:b, :], a, b - a, s_fx[q])
            for q in range(NQ):
                store(e, q)
            e.wait_ge(s["outs"], 16 * (NQ + 1))

        @block.gpsimd
        def _(e):
            e.memset(SRC, NB * P).then_inc(s["ms"], 1)
            e.memset(DST, 0).then_inc(s["ms"], 1)
            e.memset(TWv, 0.0).then_inc(s["ms"], 1)
            e.iota(iof[:, :], pattern=[[1, P]], base=0, channel_multiplier=0,
                   allow_small_or_imprecise_dtypes=True).then_inc(s["io"], 1)
            e.iota(pidx[:, :], pattern=[[0, 1]], base=0, channel_multiplier=1,
                   allow_small_or_imprecise_dtypes=True).then_inc(s["io"], 1)
            e.memset(ones[:, :], 1.0).then_inc(s["io"], 1)
            e.memset(onesf[:, :], 1.0).then_inc(s["io"], 1)
            e.memset(onef[:, :], 1.0).then_inc(s["io"], 1)
            iv = INI.rearrange("p (r w) -> p r w", w=4)
            e.memset(INI, 0).then_inc(s["cst"], 1)
            e.wait_ge(s["cst"], 1)
            e.memset(iv.bitcast(fp32)[:, :, 0:1], -1.0).then_inc(s["ini"], 1)
            e.iota(IOT[:, :, :].rearrange("p a b -> p (a b)")[:, 0:440], pattern=[[1, 440]], base=0,
                   channel_multiplier=0, allow_small_or_imprecise_dtypes=True).then_inc(s["io"], 1)
            e.wait_ge(s["zero"], 16 * 14)
            for c in range(C):
                if c % (2 * GC) == 0:
                    e.wait_ge(s["pos"], c // (2 * GC) + 1)
                e.indirect_dma_start(rec_d, bass.IndirectOffsetOnAxis(ap=IDX[:, c:c + 1], axis=0),
                                     REC[:, c, :], None).then_inc(s[f"scat{c % 4}"], 16)
            e.wait_ge(s_hq[0], 32 * (NCH // 2))
            e.wait_ge(s_hq[1], 32 * (NCH // 2))

            def gather(i, k):
                g = i * 4 + k
                for u in range(U):
                    if u == 0:
                        ge(e, s["z1"], g - 3)
                        e.wait_ge(s_rec[k], i * 16 + 16)
                        e.sem_inc(s["gt"], 1)
                    e.indirect_dma_start(G[k * U + u][:, :], None, q_d,
                                         bass.IndirectOffsetOnAxis(ap=RB[k][:, u, 1:2], axis=0))\
                     .then_inc(s_g[k * U + u], 16)
            for k in range(4):
                gather(0, k)
            with e.Fori(1, NG // 4) as i:
                for k in range(4):
                    gather(i, k)

        @block.vector
        def _(e):
            own = [0]

            def link(ins):
                own[0] += 1
                ins.then_inc(s_v, 1)
                e.wait_ge(s_v, own[0])

            e.wait_ge(s["io"], 5)
            link(e.tensor_copy(iob[:, :], iof[:, :]))
            e.tensor_scalar(identf[:, :], iof[:, :], pidx[:, :], None, ALU.is_equal)
            e.tensor_scalar(identb[:, :], iof[:, :], pidx[:, :], None, ALU.is_equal)
            link(e.tensor_scalar(Lm[:, :], iof[:, :], pidx[:, :], None, ALU.is_gt))
            e.wait_ge(s["ed"], 64)
            e.wait_ge(s["edc"], 32)
            link(e.tensor_single_scalar(IDX, SRC, 11, op=ALU.arith_shift_right))
            link(e.tensor_copy(HI, IDX))
            link(e.tensor_scalar(IDX, SRC, 7, 15, ALU.arith_shift_right, ALU.bitwise_and))
            link(e.tensor_copy(LO, IDX))
            for g in range(C // CG):
                j = g % 2
                ge(e, s["f1"], g - 1)
                for o, v, w in ((OA[j], HI, 8), (OB[j], LO, 16)):
                    ins = e.tensor_tensor(
                        o, iob[:, 0:w].rearrange("p (a w) -> p a w", a=1).broadcast_to([P, CG, w]),
                        v[:, g * CG:(g + 1) * CG].rearrange("p (c w) -> p c w", w=1).broadcast_to([P, CG, w]),
                        ALU.is_equal)
                ins.then_inc(s["o1"], 1)
            link(e.tensor_copy(hpi[:, 0:1], pidx[:, :]))
            link(e.tensor_single_scalar(hpi[:, 1:2], hpi[:, 0:1], 7, op=ALU.bitwise_and))
            link(e.tensor_single_scalar(hpi[:, 0:1], hpi[:, 0:1], 3, op=ALU.arith_shift_right))
            link(e.tensor_copy(hp[:, :], hpi[:, :]))
            iof16 = iof[:, 0:16].rearrange("p (j l) -> p j l", l=1).broadcast_to([P, 16, 16])
            link(e.tensor_scalar(MK, iof16, hp[:, 0:1], None, ALU.is_equal))
            link(e.tensor_single_scalar(IDX, SRC, 7, op=ALU.arith_shift_right))
            e.memset(BK[:, C:C + 2 * GC], 0.0)
            link(e.tensor_copy(BK[:, 0:C], IDX))
            link(e.tensor_single_scalar(IDX, SRC, 127, op=ALU.bitwise_and))
            e.tensor_copy(REC[:, :, 0:1].bitcast(fp32), IDX.rearrange("p (c w) -> p c w", w=1))
            e.tensor_copy(REC[:, :, 1:2], DST.rearrange("p (c w) -> p c w", w=1))
            link(e.tensor_copy(REC[:, :, 2:3].bitcast(fp32), TWv.rearrange("p (c w) -> p c w", w=1)))
            link(e.memset(REC[:, :, 3:4], 0))
            link(e.memset(SQ[:, :, :], 0.0))
            iota_b = iob[:, 0:NBIN].rearrange("p (a w) -> p a w", a=1).broadcast_to([P, GC, NBIN])

            def onehot(j, g):
                bk = BK[:, ds(g * GC, GC)].rearrange("p (c w) -> p c w", w=1).broadcast_to([P, GC, NBIN])
                return e.tensor_tensor(OH[j][:, :, :], iota_b, bk, ALU.is_equal)

            e.wait_ge(s["hist"], 1)
            link(e.tensor_tensor(M1, banks[0][:, 0:256].rearrange("p (j l) -> p j l", l=16), MK, ALU.mult))
            link(e.tensor_reduce(RR, M1.rearrange("p j l -> p l j"), axis=AX.X, op=ALU.add))
            hm = MK.rearrange("p j l -> p (j l)")[:, 0:128].rearrange("p (h l) -> p h l", l=16)
            iof8 = iof[:, 0:8].rearrange("p (j l) -> p j l", l=1).broadcast_to([P, 8, 16])
            link(e.tensor_scalar(hm, iof8, hp[:, 1:2], None, ALU.is_equal))
            e.tensor_tensor(hm, hm, RR.rearrange("p (a l) -> p a l", a=1).broadcast_to([P, 8, 16]), ALU.mult)\
             .then_inc(s["rr"], 1)
            e.wait_ge(s["hc"], 1)
            link(e.tensor_copy(cnt[0][:, :], banks[0][:, 0:NB]))
            link(e.tensor_scalar(cnti[:, :], cnt[0][:, :], float(P - 1), None, ALU.add))
            link(e.tensor_single_scalar(cnti[:, :], cnti[:, :], 7, op=ALU.arith_shift_right))
            link(e.tensor_copy(cnt[0][:, :], cnti[:, :]))
            a, b, d = 0, 1, 1
            while d < NB:
                e.tensor_copy(cnt[b][:, 0:d], cnt[a][:, 0:d])
                link(e.tensor_tensor(cnt[b][:, d:NB], cnt[a][:, d:NB], cnt[a][:, 0:NB - d], ALU.add))
                a, b, d = b, a, 2 * d
            e.memset(BASE[0][:, 0:1], 0.0)
            e.memset(BASE[0][:, NB:NBIN], float(NT * P))
            link(e.tensor_scalar(BASE[0][:, 1:NB], cnt[a][:, 0:NB - 1], float(P), None, ALU.mult))
            e.sem_inc(s["hs"], 1)
            for j in range(2):
                e.wait_ge(s["p2"], j + 1)
                onehot(j, j).then_inc(s["o2"], 1)
            v0 = own[0]
            NV = 15
            with e.Fori(0, NI) as i:
                n = [0]

                def lk(ins):
                    n[0] += 1
                    ins.then_inc(s_v, 1)

                def at(k):
                    e.wait_ge(s_v, i * NV + (v0 + k))

                for j in range(2):
                    g = i * 2 + j
                    e.wait_ge(s["p2"], g + 3)
                    bs = BASE[j][:, :].rearrange("p (a w) -> p a w", a=1).broadcast_to([P, GC, NBIN])
                    ps = banks[1 + j][:, 0:GC * NBIN].rearrange("p (c w) -> p c w", c=GC)
                    lk(e.tensor_tensor(TT[j][:, :, :], ps, bs, ALU.add))
                    e.wait_ge(s["o2"], g + 1)
                    at(n[0])
                    lk(e.tensor_tensor(TT[j][:, :, :], TT[j][:, :, :], OH[j][:, :, :], ALU.mult))
                    lk(e.tensor_tensor(BASE[1 - j][:, :], banks[3 + j][:, 0:NBIN], BASE[j][:, :], ALU.add))
                    at(n[0])
                    e.sem_inc(s["d2"], 1)
                    onehot(j, g + 2).then_inc(s["o2"], 1)
                    lk(e.tensor_reduce(posf[j][:, :], TT[j][:, :, :], axis=AX.X, op=ALU.add))
                    at(n[0])
                    lk(e.tensor_copy(posi[:, j * GC:(j + 1) * GC], posf[j][:, :]))
                at(n[0])
                lk(e.tensor_single_scalar(qa[:, :], posi[:, :], 0x7FFFFE00, op=ALU.bitwise_and))
                lk(e.tensor_scalar(qb[:, :], posi[:, :], 127, 2, ALU.bitwise_and, ALU.logical_shift_left))
                at(n[0])
                lk(e.tensor_tensor(qa[:, :], qa[:, :], qb[:, :], ALU.bitwise_or))
                at(n[0])
                lk(e.tensor_scalar(qb[:, :], posi[:, :], 7, 3, ALU.arith_shift_right, ALU.bitwise_and))
                at(n[0])
                lk(e.tensor_tensor(IDX[:, ds(i * (2 * GC), 2 * GC)], qa[:, :], qb[:, :], ALU.bitwise_or))
                at(n[0])
                e.sem_inc(s["pos"], 1)
                assert n[0] == NV
            own[0] += NV * NI
            e.wait_ge(s["cc"], 1)
            link(e.tensor_copy(ccol[0:NB, :], banks[0][0:NB, 0:1]))
            e.wait_ge(s["io"], 6)
            for k in range(4):
                ge(e, s["mb"], k)
                link(e.tensor_scalar(ccol[0:NB, :], ccol[0:NB, :], -440.0 if k else 0.0, None, ALU.add))
                e.tensor_scalar(MT[0:NB, :, :].rearrange("p a b -> p (a b)")[:, 0:440],
                                IOT[0:NB, :, :].rearrange("p a b -> p (a b)")[:, 0:440],
                                ccol[0:NB, :], None, ALU.is_ge).then_inc(s["m"], 1)
                e.wait_ge(s["mb"], k + 1)
                link(e.tensor_scalar(BT[0:1, k * 440:(k + 1) * 440], banks[0][0:1, 0:440],
                                     float(NB - 1), float(HF), ALU.min, ALU.mult))
            e.wait_ge(s["w"], 16 * 11)
            cur = b2_bc
            for q in range(3):
                e.tensor_scalar(msk[:, q:q + 1], pidx[:, :], float(q), None, ALU.is_equal)
                link(e.tensor_copy(b2s[:, q, :], cur[:, :]))
                if q < 2:
                    link(e.tensor_tensor(b2r[:, :], cur[:, :], b2s[:, q, :], ALU.subtract))
                    cur = b2r
            for q in range(3):
                link(e.tensor_scalar(b2s[:, q, :], b2s[:, q, :], msk[:, q:q + 1], None, ALU.mult))
            link(e.tensor_tensor(b2s[:, 0, :], b2s[:, 0, :], b2s[:, 1, :], ALU.add))
            link(e.tensor_tensor(b2s[:, 0, :], b2s[:, 0, :], b2s[:, 2, :], ALU.add))
            link(e.tensor_copy(B2[:, :, :], b2s[:, 0:1, :].broadcast_to([P, U, HF])))
            def bc(t):
                return t.rearrange("p (b f) -> p b f", f=1).broadcast_to([P, CB, NF])

            for q in range(NCH):
                X = XC[q % 2]
                nx = sum(16 * (1 + (r == NCH - 1)) for r in range(q % 2, q + 1, 2))
                e.wait_ge(s_x[q % 2], nx)
                link(e.tensor_reduce(st[:, 0, :], X[:, :, :], axis=AX.X, op=ALU.add))
                link(e.tensor_scalar(st[:, 1, :], st[:, 0, :], 1.0 / NF, None, ALU.mult))
                link(e.tensor_tensor(XM[:, :, :], X[:, :, :], bc(st[:, 1, :]), ALU.subtract))
                e.sem_inc(s["xm"], 1)
                if q == NCH - 3:
                    e.memset(X[:, CB - 1, :], 0.0).then_inc(s["ms"], 1)
                link(e.tensor_tensor(SQ[:, :, :], XM[:, :, :], XM[:, :, :], ALU.mult))
                link(e.tensor_reduce(st[:, 2, :], SQ[:, :, :], axis=AX.X, op=ALU.add))
                e.tensor_scalar(st[:, 2, :], st[:, 2, :], 1.0 / NF, EPS, ALU.mult, ALU.add).then_inc(s["var"], 1)
                e.wait_ge(s["rt"], q + 1)
                link(e.reciprocal(st[:, 3, :], st[:, 3, :]))
                link(e.tensor_tensor(XM[:, :, :], XM[:, :, :], bc(st[:, 3, :]), ALU.mult))
                ge(e, s["t1"], q - 1)
                e.tensor_scalar(H[q % 2][:, :, :], XM[:, :, :], 0.0, None, ALU.max).then_inc(s["h"], 1)
                for b in range(CB):
                    B = q * CB + b
                    e.wait_ge(s["qc"], B + 1)
                    o = HF * B
                    pq = banks[4 + B % 2]
                    e.tensor_tensor(RS[B % 2][:, :], pq[:, 0:HF], P3[0][:, o:o + HF], ALU.subtract).then_inc(s["r1"], 1)
                    e.wait_ge(s["p2c"], B + 1)
                    e.tensor_tensor(P3[2][:, o:o + HF], RS[B % 2][:, :],
                                    P3[1][:, o:o + HF], ALU.subtract).then_inc(s["p3"], 1)
            for k in range(4):
                e.wait_ge(s[f"scat{k}"], 16 * (C // 4))
            e.memset(AGG[:, :], 0.0).then_inc(s["ad"], 1)

            def build(g, k, n):
                e.wait_ge(s_rec[k], n * 16 + 16)
                ge(e, s["tp"], g - 3)
                ge(e, s["of"], g - 3)
                for u in range(U):
                    ins = e.tensor_scalar(OHb[k][:, u, :], iob[:, :], RB[k][:, u, 0:1].bitcast(fp32),
                                          None, ALU.is_equal)
                ins.then_inc(s["oh"], 1)

            def weigh(i, k):
                for u in range(U):
                    e.wait_ge(s_g[k * U + u], i * 16 + 16)
                    ins = e.scalar_tensor_tensor(out=G[k * U + u][:, :], in0=c_bc[:, :],
                                                 scalar=RB[k][:, u, 2:3].bitcast(fp32),
                                                 in1=G[k * U + u][:, :], op0=ALU.mult, op1=ALU.add)
                ins.then_inc(s["st"], 1)

            def add(g, k):
                e.wait_ge(s["ap"], g + 1)
                vs = blocks(g, mybir.EngineType.DVE)
                for u, v in enumerate(vs):
                    e.wait_ge(s["ad"], g * U + (u + 1))
                    e.tensor_tensor(AGG[:, ds(v, P)], banks[6 + k % 2][:, u * P:(u + 1) * P],
                                    AGG[:, ds(v, P)], ALU.add).then_inc(s["ad"], 1)

            build(0, 0, 0)
            for k in range(4):
                build(k + 1, (k + 1) % 4, (k + 1) // 4)
                weigh(0, k)
                if k >= 2:
                    add(k - 2, k - 2)
            with e.Fori(1, NG // 4 - 1) as i:
                for k in range(4):
                    build(i * 4 + (k + 1), (k + 1) % 4, i + (k + 1) // 4)
                    weigh(i, k)
                    add(i * 4 + (k - 2), k % 4)
            i = NG // 4 - 1
            for k in range(4):
                if k < 3:
                    build(i * 4 + (k + 1), k + 1, i)
                weigh(i, k)
                add(i * 4 + (k - 2), k % 4)
            for g in (NG - 2, NG - 1):
                add(g, g % 4)
            def bias(q):
                a, b = q * QB, min(NB, (q + 1) * QB)
                e.wait_ge(s_fx[q], 32 + 16 * (b == NB))
                for lo, hi, rows in ((a, min(b, NB - 1), P), (NB - 1, b, LAST)):
                    if lo < hi:
                        nbb = nb2_bc[0:rows, :].rearrange("p (a f) -> p a f", a=1).broadcast_to([rows, hi - lo, NF])
                        e.tensor_tensor(XA[0:rows, lo:hi, :], XA[0:rows, lo:hi, :], nbb, ALU.add).then_inc(s["fb"], 1)

            for q in range(NQ):
                bias(q)
            for q, nb in enumerate(nchunk):
                e.wait_ge(s["fu"], q + 1)
                a = 4 * q
                e.wait_ge(s["fb"], min(NQ, (a + nb - 1) // QB + 1) + (a + nb == NB))
                z = banks[2 + q % 4][:, 0:nb * NF].rearrange("p (b f) -> p b f", f=NF)
                full_b = nb - (a + nb == NB)
                if full_b:
                    ins = e.tensor_tensor(XA[:, a:a + full_b, :], z[:, 0:full_b, :], XA[:, a:a + full_b, :], ALU.add)
                if full_b < nb:
                    ins = e.tensor_tensor(XA[0:LAST, NB - 1, :], z[0:LAST, full_b, :], XA[0:LAST, NB - 1, :], ALU.add)
                ins.then_inc(s["fo"], 1)

        @block.tensor
        def _(e):
            e.wait_ge(s["io"], 5)
            for g in range(C // CG):
                e.wait_ge(s["o1"], g + 1)
                for m in range(CG // 16):
                    n = g * (CG // 16) + m
                    last = e.matmul(banks[0][:, 0:256], OA[g % 2][:, 16 * m:16 * m + 16, :].rearrange("p c h -> p (c h)"),
                                    OB[g % 2][:, 16 * m:16 * m + 16, :].rearrange("p c l -> p (c l)"),
                                    start=(n == 0), stop=(n == C // 16 - 1))
                last.then_inc(s["f1"], 1)
            e.wait_ge(s["f1"], C // CG)
            e.sem_inc(s["hist"], 1)
            e.wait_ge(s["rr"], 1)
            e.matmul(banks[0][:, 0:128], onesf[:, :], MK.rearrange("p j l -> p (j l)")[:, 0:128],
                     start=True, stop=True).then_inc(s["hc"], 1)
            e.sem_inc(s["p2"], 2)
            e.sem_inc(s["d2"], 2)
            W = NBIN
            with e.Fori(0, NI) as i:
                for j in range(2):
                    oh = OH[j][:, :, :].rearrange("p a b -> p (a b)")
                    e.wait_ge(s["o2"], i * 2 + (j + 1))
                    e.wait_ge(s["d2"], i * 2 + (j + 1))
                    ps, tot = banks[1 + j], banks[3 + j]
                    for c in range(GC):
                        e.matmul(tot[:, 0:W], ones[:, :], oh[:, c * W:(c + 1) * W], start=(c == 0), stop=(c == GC - 1))
                    e.matmul(ps[:, 0:GC * W], Lm[:, :], oh, start=True, stop=False)
                    for c in range(1, GC):
                        last = e.matmul(ps[:, c * W:GC * W], ones[:, :], oh[:, 0:(GC - c) * W],
                                        start=False, stop=(c == GC - 1))
                    last.then_inc(s["p2"], 1)
            e.wait_ge(s["hs"], 1)
            e.matmul(banks[0][0:NB, 0:1], cnt[1][0:1, :], onef[:, :], start=True, stop=True).then_inc(s["cc"], 1)
            for k in range(4):
                e.wait_ge(s["m"], k + 1)
                e.matmul(banks[0][0:1, 0:440], ones[0:NB, 0:1],
                         MT[0:NB, :, :].rearrange("p a b -> p (a b)")[:, 0:440],
                         start=True, stop=True).then_inc(s["mb"], 1)
            e.wait_ge(s["w"], 16 * 11)
            for q in range(NCH):
                e.wait_ge(s["h"], q + 1)
                for hb in range(2):
                    ge(e, s["ht"], 2 * q - 1 + hb)
                    bs = range(4 * hb, min(CB, 4 * hb + 4))
                    for b in bs:
                        last = e.matmul(banks[6 + hb][0:NF, (b - 4 * hb) * P:(b - 4 * hb + 1) * P],
                                        H[q % 2][:, b, :], identf[:, :], start=True, stop=True)
                    last.then_inc(s["t1"] if hb else s["hd"], 1)
                e.wait_ge(s["ht"], 2 * (q + 1))
                for b in range(CB):
                    B = q * CB + b
                    ge(e, s["r1"], B - 1)
                    ge(e, s["qc"], B - 1)
                    e.matmul(banks[4 + B % 2][:, 0:2 * HF], HT[q % 2][:, b * P:(b + 1) * P],
                             W1ab[:, :, :].rearrange("p a b -> p (a b)"), start=True, stop=True).then_inc(s["pq"], 1)

            def mA(g, k):
                e.wait_ge(s["oh"], g + 1)
                ge(e, s["oT"], g - 1)
                tp = TPb[k % 2]
                for u in range(U):
                    last = e.transpose(tp[:, u * P:(u + 1) * P], OHb[k][:, u, :], identb[:, :])
                last.then_inc(s["tp"], 1)

            def mB(g, k):
                vs = blocks(g, mybir.EngineType.PE)
                e.wait_ge(s["oT"], g + 1)
                e.wait_ge(s["st"], g + 1)
                ge(e, s["e1"], g - 1)
                for u, v in enumerate(vs):
                    z = banks[2 + k % 2][:, u * P:(u + 1) * P]
                    e.matmul(z, G[k * U + u][:, :], identf[:, :], start=True, stop=False)
                    for q in range(3):
                        last = e.matmul(z, P3[q][:, ds(v, HF)], OHT[k % 2][:, u * P:(u + 1) * P],
                                        start=False, stop=(q == 2))
                last.then_inc(s["z1"], 1)

            def mC(g, k):
                e.wait_ge(s["e1"], g + 1)
                ge(e, s["e2"], g - 1)
                z = banks[4 + k % 2]
                e.matmul(z[:, :], ones[:, :], B2[:, :, :].rearrange("p a b -> p (a b)"), start=True, stop=False)
                for u in range(U):
                    last = e.matmul(z[:, u * HF:(u + 1) * HF], E1[k % 2][:, u * P:(u + 1) * P], W2[:, :],
                                    start=False, stop=(u == U - 1))
                last.then_inc(s["z2"], 1)

            def mD(g, k):
                e.wait_ge(s["e2"], g + 1)
                e.wait_ge(s["of"], g + 1)
                ge(e, s["ad"], (g - 1) * U + 1)
                for u in range(U):
                    last = e.matmul(banks[6 + k % 2][:, u * P:(u + 1) * P], E2[k % 2][:, u * HF:(u + 1) * HF],
                                    OHf[k][:, u, :], start=True, stop=True)
                last.then_inc(s["ap"], 1)

            e.wait_ge(s["p3"], NB)
            e.wait_ge(s["qc"], NB)
            for k in range(4):
                mA(k, k)
                if k >= 2:
                    mD(k - 2, k - 2)
                if k >= 1:
                    mC(k - 1, k - 1)
                mB(k, k)
            with e.Fori(1, NG // 4) as i:
                for k in range(4):
                    g = i * 4 + k
                    mA(g, k)
                    mD(i * 4 + (k - 2), (k - 2) % 4)
                    mC(i * 4 + (k - 1), (k - 1) % 4)
                    mB(g, k)
            mD(NG - 2, (NG - 2) % 4)
            mC(NG - 1, (NG - 1) % 4)
            mD(NG - 1, (NG - 1) % 4)
            e.wait_ge(s["ad"], NT + 1)
            for q in range(len(nchunk) + 1):
                if q < len(nchunk):
                    nb = nchunk[q]
                    a = 4 * q
                    r1 = (a + nb - 1) // QB
                    for r0 in range(a // QB, r1 + 1):
                        e.wait_ge(s_fx[r0], 32 + 16 * (r0 == NQ - 1))
                    ge(e, s["fd"], q - 1)
                    z = banks[q % 2][:, 0:nb * P]
                    e.matmul(z, nW1b[:, :], AGG[:, q * 512:q * 512 + nb * P], start=True, stop=False)
                    e.matmul(z, nW1a[:, :], HA[:, q * 512:q * 512 + nb * P], start=False, stop=True).then_inc(s["fz"], 1)
                if q:
                    r = q - 1
                    e.wait_ge(s["fd"], r + 1)
                    ge(e, s["fo"], r - 3)
                    for b in range(nchunk[r]):
                        last = e.matmul(banks[2 + r % 4][:, b * NF:(b + 1) * NF], E1[r % 2][:, b * P:(b + 1) * P],
                                        nW2s[:, :], start=True, stop=True)
                    last.then_inc(s["fu"], 1)

        @block.scalar
        def _(e):
            e.wait_ge(s["ms"], 3)
            ewf = ew.rearrange("n a -> (n a)")
            e.dma_start(TWv[0:P - 1, :], ewf[0:full].rearrange("(p c) -> p c", c=C)).then_inc(s["edc"], 16)
            e.dma_start(TWv[P - 1:P, 0:LASTC], ewf[full:E].rearrange("(p c) -> p c", c=LASTC)).then_inc(s["edc"], 16)
            for q in range(NCH):
                e.wait_ge(s["var"], q + 1)
                e.activation(st[:, 3, :], st[:, 2, :], ACT.Sqrt).then_inc(s["rt"], 1)
                if q >= 2:
                    e.wait_ge(s_hq[q % 2], 32 * (q // 2))
                for hb in range(2):
                    e.wait_ge(s["t1"] if hb else s["hd"], q + 1)
                    n = (4 - hb) * P
                    e.activation(HT[q % 2][:, hb * 512:hb * 512 + n], banks[6 + hb][0:NF, 0:n],
                                 ACT.Copy).then_inc(s["ht"], 1)
                for b in range(CB):
                    B = q * CB + b
                    o = HF * B
                    e.wait_ge(s["pq"], B + 1)
                    pq = banks[4 + B % 2]
                    e.activation(P3[0][:, o:o + HF], pq[:, 0:HF], ACT.Copy).then_inc(s["p1"], 1)
                    e.activation(QS[q % 2][:, b, :], pq[:, HF:2 * HF], ACT.Copy).then_inc(s["qc"], 1)
                    e.wait_ge(s["r1"], B + 1)
                    e.activation(P3[1][:, o:o + HF], RS[B % 2][:, :], ACT.Copy).then_inc(s["p2c"], 1)

            def tcopy(g, k):
                e.wait_ge(s["tp"], g + 1)
                ge(e, s["z1"], g - 1)
                e.activation(OHT[k % 2][:, :], TPb[k % 2], ACT.Copy).then_inc(s["oT"], 1)
                ge(e, s["ap"], g - 3)
                e.activation(OHf[k][:, :, :], OHb[k][:, :, :], ACT.Copy).then_inc(s["of"], 1)

            def silu1(g, k):
                e.wait_ge(s["z1"], g + 1)
                ge(e, s["z2"], g - 1)
                e.activation(E1[k % 2][:, :], banks[2 + k % 2][:, :], ACT.Silu, bias=eb1c[:, :]).then_inc(s["e1"], 1)

            def silu2(g, k):
                e.wait_ge(s["z2"], g + 1)
                ge(e, s["ap"], g - 1)
                e.activation(E2[k % 2][:, :], banks[4 + k % 2][:, :], ACT.Silu).then_inc(s["e2"], 1)

            e.wait_ge(s["w"], 16 * 11)
            for k in range(4):
                tcopy(k, k)
                if k:
                    silu2(k - 1, k - 1)
                silu1(k, k)
            with e.Fori(1, NG // 4) as i:
                for k in range(4):
                    g = i * 4 + k
                    tcopy(g, k)
                    silu2(i * 4 + (k - 1), (k - 1) % 4)
                    silu1(g, k)
            silu2(NG - 1, (NG - 1) % 4)
            for q, nb in enumerate(nchunk):
                e.wait_ge(s["fz"], q + 1)
                ge(e, s["fu"], q - 1)
                e.activation(E1[q % 2][:, 0:nb * P], banks[q % 2][:, 0:nb * P], ACT.Silu, bias=nb1c[:, :])\
                 .then_inc(s["fd"], 1)


_INS = ["x", "src", "dst", "edge_weight1", "L0_gnn_eW1", "L0_gnn_eb1", "L0_gnn_eW2", "L0_gnn_eb2",
        "L0_gnn_nW1", "L0_gnn_nb1", "L0_gnn_nW2", "L0_gnn_nb2"]


def kernel(**inputs):
    import numpy as _np
    import concourse.bacc as _bacc
    from concourse import mybir as _mybir
    from concourse.bass_utils import run_bass_kernel_spmd as _run

    nc = _bacc.Bacc("TRN2", target_bir_lowering=False, num_devices=1)
    arrays, args = {}, []
    for name in _INS:
        a = _np.ascontiguousarray(inputs[name])
        arrays[f"in_{name}"] = a
        args.append(nc.dram_tensor(f"in_{name}", a.shape, _mybir.dt.from_np(a.dtype), kind="ExternalInput").ap())
    out = nc.dram_tensor("out_0", (N, NF), _mybir.dt.float32, kind="ExternalOutput").ap()
    gnn(nc, *args, out)
    return _run(nc, [arrays], core_ids=[0]).results[0]["out_0"]
```

```python
import concourse.bass as bass
from concourse import mybir
from contextlib import ExitStack

N, NF, HF = 12500, 64, 128
E = 212500
P = 128
NB = (N + P - 1) // P
NPAD = NB * P
LAST = N - (NB - 1) * P
NBIN = NB + 1
C = 1664
LASTC = E - (P - 1) * C
GC = 4
SC = 32
NS = C // SC
LR = 1
R = 1 << LR
CHB = (SC * P + NBIN * (R - 1)) // (R * P) + 1
CH = CHB * P
CW = CHB * R
U = 4
NG = 449
NT = NG * U
TRASH = NT * P // R
CPT = P // R
EPS = 1e-5


def ge(eng, sem, val):
    if not isinstance(val, int) or val > 0:
        eng.wait_ge(sem, val)


def gnn(nc, x, src, dst, ew, eW1, eb1, eW2, eb2, nW1, nb1, nW2, nb2, out):
    fp32, bf16, i32 = mybir.dt.float32, mybir.dt.bfloat16, mybir.dt.int32
    ALU, ACT, AX = mybir.AluOpType, mybir.ActivationFunctionType, mybir.AxisListType
    ds = bass.ds

    rec_d = nc.dram_tensor("rec_d", (TRASH + NS * CH, R * 4), i32).ap()
    rows_d = rec_d[0:TRASH, :].rearrange("c (r w) -> (c r) w", w=4)
    q_d = nc.dram_tensor("q_d", (NPAD, HF), fp32).ap()
    hT_d = nc.dram_tensor("hT_d", (NF, NPAD), fp32).ap()

    with ExitStack() as ctx:
        def sb(name, shape, dt):
            return ctx.enter_context(nc.sbuf_tensor(name, shape, dt))

        def sem(name):
            return ctx.enter_context(nc.semaphore(name))

        iof = sb("iof", [P, P], fp32)
        iob = sb("iob", [P, P], bf16)
        pidx = sb("pidx", [P, 1], fp32)
        identf = sb("identf", [P, P], fp32)
        identb = sb("identb", [P, P], bf16)
        ones = sb("ones", [P, P], bf16)
        onef = sb("onef", [1, 1], fp32)
        Lm = sb("Lm", [P, P], bf16)
        onesf = sb("onesf", [P, P], fp32)
        hp = sb("hp", [P, 2], fp32)
        hpi = sb("hpi", [P, 2], i32)
        W1ab = sb("W1ab", [NF, 2, HF], fp32)
        c_bc = sb("c_bc", [P, HF], fp32)
        b2_bc = sb("b2_bc", [P, HF], fp32)
        b2s = sb("b2s", [P, 3, HF], bf16)
        b2r = sb("b2r", [P, HF], fp32)
        msk = sb("msk", [P, 3], fp32)
        B2 = sb("B2", [P, U, HF], bf16)
        W2 = sb("W2", [HF, HF], fp32)
        eb1c = sb("eb1c", [HF, 1], fp32)
        nb1c = sb("nb1c", [HF, 1], fp32)
        nW1a = sb("nW1a", [NF, HF], fp32)
        nW1b = sb("nW1b", [HF, HF], fp32)
        nW2s = sb("nW2s", [HF, NF], fp32)
        nb2_bc = sb("nb2_bc", [P, NF], fp32)
        P3all = sb("P3", [P, 3 * NPAD], bf16)
        P3 = [P3all[:, q * NPAD:(q + 1) * NPAD] for q in range(3)]
        XA = P3all[:, 0:2 * NB * NF].bitcast(fp32).rearrange("p (b f) -> p b f", f=NF)
        HA = P3all[0:NF, 2 * NB * NF:2 * NB * NF + 2 * NPAD].bitcast(fp32)
        BIG = sb("BIG", [P, NPAD], fp32)
        AGG = BIG
        def part(a, n):
            return BIG[:, a:a + n]
        VAL = part(0, 2 * C).rearrange("p (c w) -> p c w", w=2)
        SRC = part(2 * C, C).bitcast(i32)
        DST = part(3 * C, C).bitcast(i32)
        AO = [part(2 * C + k * GC * P, GC * P).rearrange("p (c a) -> p c a", a=P) for k in range(4)]
        o1 = 2 * C + 4 * GC * P
        BV = [part(o1 + k * 16 * CW, 16 * CW).rearrange("p (c v b) -> p c v b", v=2, b=CW) for k in range(2)]
        assert o1 + 32 * CW <= 4 * C
        o1 = 4 * C
        OHB = [part(o1 + k * 8 * CW, 8 * CW).rearrange("p (c b) -> p c b", b=CW) for k in range(2)]
        o1 += 16 * CW
        T32 = part(o1, C).bitcast(i32)
        MM = BIG[:, o1:o1 + CH].bitcast(bf16)[:, 0:CH]
        o1 += CH // 2
        AB = [part(o1 + k * GC * P, GC * P).rearrange("p (c a) -> p c a", a=P) for k in range(2)]
        o1 += 2 * GC * P
        SCR = part(o1, 2 * GC * NBIN).rearrange("p (k c b) -> p k c b", k=2, b=NBIN)
        o1 += 2 * GC * NBIN
        OREC = o1
        REC = [part(o1 + k * CW * 4, CW * 4).bitcast(i32) for k in range(4)]
        assert o1 + 16 * CW <= NPAD
        TWv = P3all[:, 0:2 * C].bitcast(fp32)
        CG = 64
        HI, LO = (P3all[:, a * C:(a + 1) * C] for a in (2, 3))
        o1 = 4 * C
        OA = [P3all[:, o1 + j * CG * 8:o1 + (j + 1) * CG * 8].rearrange("p (c h) -> p c h", h=8) for j in range(2)]
        o1 += 2 * CG * 8
        OB = [P3all[:, o1 + j * CG * 16:o1 + (j + 1) * CG * 16].rearrange("p (c l) -> p c l", l=16) for j in range(2)]
        o1 += 2 * CG * 16
        M1 = P3all[0:32, o1:o1 + 512].bitcast(fp32).rearrange("p (s j l) -> p s j l", j=4, l=16)
        MK = P3all[0:32, o1 + 512:o1 + 640].bitcast(fp32).rearrange("p (j l) -> p j l", l=16)
        RR = P3all[0:32, o1 + 640:o1 + 768].bitcast(fp32).rearrange("p (s l) -> p s l", l=16)
        HMK = P3all[0:32, o1 + 768:o1 + 1024].bitcast(fp32).rearrange("p (h l) -> p h l", l=16)
        HM = [P3all[0:32, o1 + 1024 * j:o1 + 1024 * (j + 1)].bitcast(fp32) for j in (1, 2)]
        BT = sb("BT", [1, NT], i32)
        BK = sb("BK", [P, C], bf16)
        GA = sb("GA", [P, 4 * U * HF], fp32)
        used = [0]

        def ga(shape, dt):
            o, used[0] = used[0], used[0] + shape[1]
            assert used[0] <= 4 * U * HF
            t = GA[:, o:o + shape[1]]
            return t if dt == fp32 else t.bitcast(dt)

        OH = [[sb(f"OH{j}_{k}", [P, GC, NBIN], bf16) for k in range(4)] for j in range(2)]
        CY = [[sb(f"CY{j}_{k}", [P, 2, NBIN], bf16) for k in range(2)] for j in range(2)]
        Lf = ga([P, P], fp32)
        DM = ga([P, P], fp32)
        LB = [ga([P, P], fp32) for j in range(2)]
        nI = ga([P, NS], i32)
        ccT = ga([P, NS], fp32)
        lbT = ga([P, NS], fp32)
        lbR = ga([P, NS], fp32)
        gA = [ga([P, NS], fp32) for j in range(2)]
        dl = ga([P, NS], fp32)
        dd = ga([P, NS], fp32)
        dd3 = sb("dd3", [P, NS, 3], bf16)
        dsum = sb("dsum", [P, CHB], fp32)
        SI = ga([P, NS], fp32)
        lbn = ga([P, NS], fp32)
        IDX = [ga([P, CHB], i32) for k in range(4)]
        cl = ga([P, 8], fp32)
        cli = ga([P, 1], i32)
        POS = [ga([P, 2 * SC], fp32) for k in range(2)]
        AF = [ga([P, 2 * SC], fp32) for k in range(2)]
        AFn = [ga([P, 2 * SC], fp32) for k in range(2)]
        BF = [ga([P, 2 * SC], fp32) for k in range(2)]
        PI = ga([P, 2 * SC], i32)
        i1 = ga([P, 2 * SC], i32)
        i2 = ga([P, 2 * SC], i32)
        i3 = ga([P, 2 * SC], i32)
        pki = ga([P, CW], i32)
        shi = ga([P, CW], i32)
        CB = 7
        NCH = NB // CB
        XC = [sb(f"XC{j}", [P, CB, NF], fp32) for j in range(2)]
        XM = sb("XM", [P, CB, NF], fp32)
        SQ = sb("SQ", [P, CB, NF], fp32)
        H = [sb(f"H{j}", [P, CB, NF], fp32) for j in range(2)]
        st = sb("st", [P, 4, CB], fp32)
        HT = [sb(f"HT{j}", [NF, CB * P], fp32) for j in range(2)]
        QS = [sb(f"QS{j}", [P, CB, HF], fp32) for j in range(2)]
        RS = [sb(f"RS{j}", [P, HF], fp32) for j in range(2)]
        RB = [sb(f"RB{k}", [P, U, 4], i32) for k in range(4)]
        G = [GA[:, k * HF:(k + 1) * HF] for k in range(4 * U)]
        OHb = [sb(f"OHb{k}", [P, U, P], bf16) for k in range(4)]
        OHT = [sb(f"OHT{k}", [P, U * P], bf16) for k in range(2)]
        ED = sb("ED", [P, 8 * 512], fp32)
        OHf = [ED[:, k * 512:(k + 1) * 512].rearrange("p (u a) -> p u a", a=P) for k in range(4)]
        E1 = [ED[:, (4 + k) * 512:(5 + k) * 512] for k in range(2)]
        E2 = [ED[:, (6 + k) * 512:(7 + k) * 512] for k in range(2)]
        F1 = E1 + E2
        IOJ = ED[:, 0:CH]
        IR = (NT + 15) // 16
        INI = ED[:, 3072:3072 + IR * 4].bitcast(i32)
        DCI = ED[:, CH:CH + NS * CHB].rearrange("p (s m) -> p s m", m=CHB)
        IOT = ED[:, 3584:3584 + NG]
        MT = OHb[1]

        banks = [ctx.enter_context(nc.psum_tensor(f"bk{i}", [P, 512], fp32)) for i in range(8)]

        TPb = [banks[k][:, :].bitcast(bf16)[:, 0:512] for k in range(2)]

        names = ("rr hc fb cst io w ms ed edc o1 f1 cc lb tl tb df dq m mb o2 p2 tt lbb cr ch cy vw ps bv a0 ab a1 so mm dd dr up rec "
                 "xm sq h t1 ht pq p1 r1 p2c p3 qc fin htd qd ini scat0 scat1 scat2 scat3 "
                 "gt oh st ad tp z1 z2 ap oT of e1 e2 zero var rt hd fz fu fo fd outs one").split()
        s = {n: sem("s_" + n) for n in names}
        s_x = [sem(f"s_x{j}") for j in range(2)]
        s_hq = [sem(f"s_hq{j}") for j in range(2)]
        s_rec = [sem(f"s_rec{k}") for k in range(4)]
        s_g = [sem(f"s_g{k}") for k in range(4 * U)]
        QB = 12
        NQ = (NB + QB - 1) // QB
        s_fx = [sem(f"s_fx{k}") for k in range(NQ)]
        s_v = sem("s_v")
        NW = 12

        def blocks(g, engine):
            return nc.values_load_multi_w_load_instructions(
                BT[0:1, ds(g * U, U)], engines=[engine], min_val=0, max_val=(NB - 1) * P,
                skip_runtime_bounds_check_because="BT is clipped to them when it is made")[1]

        block = ctx.enter_context(nc.Block())
        NU = 2 * SC // GC
        NR = NS // 2 * NU
        WC = GC * NBIN
        OFF = NU + 2

        def unit(n):
            return n // NU * 2 + n % 2, n % NU // 2 * GC

        def carries(n):
            return n // NU * (NU - 2) + n % NU

        def node_steps(parts):
            at = {}
            for q in range(NCH):
                t0 = 14 + 28 * q
                for name, off, f in parts:
                    if off is None:
                        for b in range(CB):
                            at.setdefault(t0 + 10 + 3 * b + name, []).append((f, q, b))
                    else:
                        at.setdefault(t0 + off, []).append((f, q, None))
            return at
        nchunk = [min(4, NB - 4 * q) for q in range((NB + 3) // 4)]
        full = (P - 1) * C

        def stage_out(e, q):
            e.wait_ge(s["ht"], 2 * (q + 1))
            e.dma_start(hT_d[:, q * CB * P:(q + 1) * CB * P], HT[q % 2][:, :]).then_inc(s_hq[q % 2], 16)
            e.wait_ge(s["qc"], CB * (q + 1))
            e.dma_start(q_d[q * CB * P:(q + 1) * CB * P, :].rearrange("(b p) f -> p b f", p=P),
                        QS[q % 2][:, :, :]).then_inc(s_hq[q % 2], 16)

        def store(e, q):
            a, b = q * QB, min(NB, (q + 1) * QB)
            e.wait_ge(s["fo"], min(len(nchunk), (b + 3) // 4))
            rows = out[a * P:min(N, b * P), :]
            k = rows.shape[0] // P
            e.dma_start(rows[0:k * P, :].rearrange("(b p) f -> p b f", p=P), XA[:, a:a + k, :])\
             .then_inc(s["outs"], 16)
            if k < b - a:
                e.dma_start(rows[k * P:, :], XA[0:LAST, a + k, :]).then_inc(s["outs"], 16)

        @block.sync
        def _(e):
            e.wait_ge(s["ms"], 3)
            for t, a in ((SRC, src), (DST, dst)):
                e.dma_start(t[0:P - 1, :], a[0:full].rearrange("(p c) -> p c", c=C)).then_inc(s["ed"], 16)
                e.dma_start(t[P - 1:P, 0:LASTC], a[full:E].rearrange("(p c) -> p c", c=LASTC)).then_inc(s["ed"], 16)
            e.wait_ge(s["ini"], 1)
            init_d = rec_d[0:16 * IR * P // R, :].rearrange("c (r w) -> (c r) w", w=4)
            for k in range(16):
                e.dma_start(init_d.rearrange("(a p r) w -> a p (r w)", a=16, p=P)[k], INI).then_inc(s["zero"], 16)
            for t, a in ((W1ab[:, 0, :], eW1[0:NF, :]), (W1ab[:, 1, :], eW1[NF:2 * NF, :]),
                         (c_bc[:, :], eW1[2 * NF:2 * NF + 1, :].broadcast_to([P, HF])),
                         (b2_bc[:, :], eb2.rearrange("(a n) -> a n", a=1).broadcast_to([P, HF])),
                         (W2[:, :], eW2), (eb1c[:, :], eb1.rearrange("(n a) -> n a", a=1)),
                         (nb1c[:, :], nb1.rearrange("(n a) -> n a", a=1)),
                         (nW1a[:, :], nW1[0:NF, :]), (nW1b[:, :], nW1[NF:NF + HF, :]), (nW2s[:, :], nW2),
                         (nb2_bc[:, :], nb2.rearrange("(a n) -> a n", a=1).broadcast_to([P, NF]))):
                e.dma_start(t, a).then_inc(s["w"], 16)

            def load_x(t, c0, nb, sm):
                rows = x[c0 * P:min(N, (c0 + nb) * P), :]
                k = rows.shape[0] // P
                e.dma_start(t[:, 0:k, :], rows[0:k * P, :].rearrange("(b p) f -> p b f", p=P)).then_inc(sm, 16)
                if k < nb:
                    e.dma_start(t[0:LAST, k, :], rows[k * P:, :]).then_inc(sm, 16)

            for q in range(NCH):
                ge(e, s["xm"], q - 1)
                if q == NCH - 1:
                    e.wait_ge(s["ms"], 4)
                load_x(XC[q % 2], q * CB, CB, s_x[q % 2])
                if q:
                    stage_out(e, q - 1)
            stage_out(e, NCH - 1)
            for k in range(4):
                e.wait_ge(s[f"scat{k}"], 16 * CHB * (NS // 4))
            rg = rows_d.rearrange("(g u p) w -> p g u w", p=P, u=U)

            def load_rec(i, k):
                g = i * 4 + k
                ge(e, s["st"], g - 3)
                ge(e, s["oh"], g - 3)
                e.dma_start(RB[k][:, :, :], rg[:, ds(g, 1), :, :].rearrange("p a u w -> p (a u) w"))\
                 .then_inc(s_rec[k], 16)
            for k in range(4):
                load_rec(0, k)
            with e.Fori(1, NG // 4) as i:
                for k in range(4):
                    load_rec(i, k)
            for k in range(NG % 4):
                load_rec(NG // 4, k)
            e.wait_ge(s["z1"], NG)
            for j in range(2):
                e.wait_ge(s_hq[j], 32 * (NCH // 2))
            for q in range(NQ):
                a, b = q * QB, min(NB, (q + 1) * QB)
                e.dma_start(HA[:, a * P:b * P], hT_d[:, a * P:b * P]).then_inc(s_fx[q], 16)
                load_x(XA[:, a:b, :], a, b - a, s_fx[q])
            for q in range(NQ):
                store(e, q)
            e.wait_ge(s["outs"], 16 * (NQ + 1))

        @block.gpsimd
        def _(e):
            e.memset(SRC, NB * P).then_inc(s["ms"], 1)
            e.memset(DST, 0).then_inc(s["ms"], 1)
            e.memset(TWv, 0.0).then_inc(s["ms"], 1)
            e.iota(iof[:, :], pattern=[[1, P]], base=0, channel_multiplier=0,
                   allow_small_or_imprecise_dtypes=True).then_inc(s["io"], 1)
            e.iota(pidx[:, :], pattern=[[0, 1]], base=0, channel_multiplier=1,
                   allow_small_or_imprecise_dtypes=True).then_inc(s["io"], 1)
            e.memset(ones[:, :], 1.0).then_inc(s["io"], 1)
            e.memset(onesf[:, :], 1.0).then_inc(s["io"], 1)
            e.memset(onef[:, :], 1.0).then_inc(s["io"], 1)
            iv = INI.rearrange("p (r w) -> p r w", w=4)
            e.memset(INI, 0).then_inc(s["cst"], 1)
            e.wait_ge(s["cst"], 1)
            e.memset(iv.bitcast(fp32)[:, :, 0:1], -1.0).then_inc(s["ini"], 1)
            for t, pat, b0, cm in ((SI[:, :], [[CH, NS]], TRASH, 0), (DCI, [[CH // 2, NS], [P, CHB]], TRASH // 2, 1),
                                   (IOT, [[1, NG]], 0, 0), (IOJ, [[1, CH]], 0, 0)):
                e.iota(t, pattern=pat, base=b0, channel_multiplier=cm,
                       allow_small_or_imprecise_dtypes=True).then_inc(s["io"], 1)
            e.wait_ge(s["zero"], 16 * 16)
            for q in range(NS):
                e.wait_ge(s["rec"], q + 1)
                for c in range(CHB):
                    e.indirect_dma_start(rec_d, bass.IndirectOffsetOnAxis(ap=IDX[q % 4][:, c:c + 1], axis=0),
                                         REC[q % 4][:, c * R * 4:(c + 1) * R * 4], None)\
                     .then_inc(s[f"scat{q % 4}"], 16)
            e.wait_ge(s_hq[0], 32 * (NCH // 2))
            e.wait_ge(s_hq[1], 32 * (NCH // 2))

            def gather(i, k):
                g = i * 4 + k
                for u in range(U):
                    if u == 0:
                        ge(e, s["z1"], g - 3)
                        e.wait_ge(s_rec[k], i * 16 + 16)
                        e.sem_inc(s["gt"], 1)
                    e.indirect_dma_start(G[k * U + u], None, q_d,
                                         bass.IndirectOffsetOnAxis(ap=RB[k][:, u, 1:2], axis=0))\
                     .then_inc(s_g[k * U + u], 16)
            for k in range(4):
                gather(0, k)
            with e.Fori(1, NG // 4) as i:
                for k in range(4):
                    gather(i, k)
            for k in range(NG % 4):
                gather(NG // 4, k)

        @block.vector
        def _(e):
            own = [0]

            def link(ins):
                own[0] += 1
                ins.then_inc(s_v, 1)
                e.wait_ge(s_v, own[0])

            def mark(ins):
                own[0] += 1
                ins.then_inc(s_v, 1)
                return own[0]

            e.wait_ge(s["io"], 5)
            link(e.tensor_copy(iob[:, :], iof[:, :]))
            e.tensor_scalar(identf[:, :], iof[:, :], pidx[:, :], None, ALU.is_equal)
            e.tensor_scalar(identb[:, :], iof[:, :], pidx[:, :], None, ALU.is_equal)
            e.tensor_scalar(Lm[:, :], iof[:, :], pidx[:, :], None, ALU.is_gt)
            e.tensor_scalar(Lf[:, :], iof[:, :], pidx[:, :], None, ALU.is_gt)
            link(e.tensor_scalar(cl[:, 0:1], pidx[:, :], 1.0, None, ALU.add))
            e.tensor_scalar(cl[:, 1:2], pidx[:, :], float(NB), None, ALU.is_lt)
            e.tensor_scalar(cl[:, 2:3], pidx[:, :], float(NB), None, ALU.is_equal)
            link(e.tensor_scalar(DM[:, :], iof[:, :], cl[:, 0:1], None, ALU.is_equal))
            link(e.tensor_tensor(DM[:, :], identf[:, :], DM[:, :], ALU.subtract))
            link(e.tensor_copy(hpi[:, 0:1], pidx[:, :]))
            link(e.tensor_single_scalar(hpi[:, 1:2], hpi[:, 0:1], 7, op=ALU.bitwise_and))
            link(e.tensor_single_scalar(hpi[:, 0:1], hpi[:, 0:1], 3, op=ALU.arith_shift_right))
            link(e.tensor_copy(hp[:, :], hpi[:, :]))
            iof4 = iof[0:32, 0:4].rearrange("p (j l) -> p j l", l=1).broadcast_to([32, 4, 16])
            link(e.tensor_scalar(MK, iof4, hp[0:32, 0:1], None, ALU.is_equal))
            iof8 = iof[0:32, 0:8].rearrange("p (j l) -> p j l", l=1).broadcast_to([32, 8, 16])
            link(e.tensor_scalar(HMK, iof8, hp[0:32, 1:2], None, ALU.is_equal))
            for k in range(4):
                link(e.memset(REC[k], 0))
            e.wait_ge(s["ed"], 64)
            link(e.tensor_single_scalar(T32, SRC, 11, op=ALU.arith_shift_right))
            link(e.tensor_copy(HI, T32))
            link(e.tensor_scalar(T32, SRC, 7, 15, ALU.arith_shift_right, ALU.bitwise_and))
            link(e.tensor_copy(LO, T32))
            def counts(r):
                e.wait_ge(s["f1"], 2 * r + 2)
                link(e.tensor_tensor(M1, banks[r % 2][0:32, 0:256].rearrange("p (s j l) -> p s j l", j=4, l=16),
                                     MK.rearrange("p (s j) l -> p s j l", s=1).broadcast_to([32, 4, 4, 16]), ALU.mult))
                link(e.tensor_reduce(RR, M1.rearrange("p s j l -> p s l j"), axis=AX.X, op=ALU.add))
                ge(e, s["hc"], 4 * (r - 1))
                e.tensor_tensor(HM[r % 2].rearrange("p (s h l) -> p s h l", s=4, h=8),
                                HMK.rearrange("p (s h) l -> p s h l", s=1).broadcast_to([32, 4, 8, 16]),
                                RR.rearrange("p s (h l) -> p s h l", h=1).broadcast_to([32, 4, 8, 16]), ALU.mult)\
                 .then_inc(s["rr"], 1)

            for g in range(C // CG):
                j = g % 2
                ge(e, s["f1"], g - 1)
                for o, v, w in ((OA[j], HI, 8), (OB[j], LO, 16)):
                    ins = e.tensor_tensor(
                        o, iob[:, 0:w].rearrange("p (a w) -> p a w", a=1).broadcast_to([P, CG, w]),
                        v[:, g * CG:(g + 1) * CG].rearrange("p (c w) -> p c w", w=1).broadcast_to([P, CG, w]),
                        ALU.is_equal)
                ins.then_inc(s["o1"], 1)
                if g and g % 2 == 0:
                    counts(g // 2 - 1)
            counts(NS // 4 - 1)
            link(e.tensor_single_scalar(T32, SRC, 7, op=ALU.arith_shift_right))
            link(e.tensor_copy(BK[:, :], T32))
            e.wait_ge(s["hc"], NS)
            link(e.tensor_scalar(nI[:, :], banks[2][:, 0:NS], float(R - 1), None, ALU.add))
            link(e.tensor_single_scalar(nI[:, :], nI[:, :], LR, op=ALU.arith_shift_right))
            link(e.tensor_copy(ccT[:, :], nI[:, :]))
            e.sem_inc(s["cc"], 1)
            link(e.memset(gA[0][:, 0:1], 0.0))
            link(e.tensor_copy(gA[0][:, 1:NS], ccT[:, 0:NS - 1]))
            a, b, d = 0, 1, 1
            while d < NS:
                e.tensor_copy(gA[b][:, 0:d], gA[a][:, 0:d])
                link(e.tensor_tensor(gA[b][:, d:NS], gA[a][:, d:NS], gA[a][:, 0:NS - d], ALU.add))
                a, b, d = b, a, 2 * d
            gs, g2 = gA[a], gA[b]
            link(e.tensor_tensor(cl[:, 3:4], gs[:, NS - 1:NS], ccT[:, NS - 1:NS], ALU.add))
            link(e.tensor_scalar(cli[:, :], cl[:, 3:4], float(CPT - 1), None, ALU.add))
            link(e.tensor_single_scalar(cli[:, :], cli[:, :], 7 - LR, op=ALU.arith_shift_right))
            link(e.tensor_scalar(cl[:, 4:5], cli[:, :], cl[:, 1:2], None, ALU.mult))
            e.sem_inc(s["tl"], 1)
            e.wait_ge(s["lb"], 1)
            link(e.tensor_copy(lbT[:, :], banks[3][:, 0:NS]))
            link(e.tensor_scalar(lbR[:, :], lbT[:, :], float(R), None, ALU.mult))
            link(e.tensor_scalar(lbn[:, :], lbT[:, :], -1.0, 0.5, ALU.mult, ALU.add))
            e.sem_inc(s["dq"], 1)
            link(e.tensor_tensor(dl[:, :], gs[:, :], lbT[:, :], ALU.subtract))
            e.wait_ge(s["tb"], 1)
            link(e.tensor_copy(cl[:, 5:6], banks[4][:, 0:1]))
            link(e.tensor_tensor(cl[:, 6:7], cl[:, 5:6], cl[:, 4:5], ALU.add))
            link(e.tensor_scalar(cl[:, 5:6], cl[:, 5:6], float(CPT), None, ALU.mult))
            link(e.tensor_scalar(dl[:, :], dl[:, :], cl[:, 5:6], cl[:, 1:2], ALU.add, ALU.mult))
            e.wait_ge(s["io"], 9)
            link(e.scalar_tensor_tensor(out=dl[:, :], in0=SI[:, :], scalar=cl[:, 2:3], in1=dl[:, :],
                                        op0=ALU.mult, op1=ALU.add))
            e.sem_inc(s["df"], 1)
            e.wait_ge(s["df"], 2)
            link(e.tensor_copy(dd[:, :], banks[3][:, 0:NS]))
            for k in range(3):
                link(e.tensor_copy(dd3[:, :, k], dd[:, :]))
                if k < 2:
                    link(e.tensor_tensor(dd[:, :], dd[:, :], dd3[:, :, k], ALU.subtract))

            iota_b = iob[:, 0:NBIN].rearrange("p (a w) -> p a w", a=1).broadcast_to([P, GC, NBIN])

            def onehot(n):
                q, c = unit(n)
                c += q * SC
                bk = BK[:, c:c + GC].rearrange("p (c w) -> p c w", w=1).broadcast_to([P, GC, NBIN])
                e.tensor_tensor(OH[n % 2][n // 2 % 4][:, :, :], iota_b, bk, ALU.is_equal).then_inc(s["o2"], 1)

            def ranks(n):
                q, c = unit(n)
                o = n % 2 * SC + c
                e.wait_ge(s["o2"], n + 1)
                e.wait_ge(s["p2"], n + 1)
                for k in range(GC):
                    ins = e.tensor_tensor_reduce(SCR[:, n % 2, k, :], banks[n % 2][:, k * NBIN:(k + 1) * NBIN],
                                                 OH[n % 2][n // 2 % 4][:, k, :], 1.0, 0.0, ALU.mult, ALU.add,
                                                 POS[n // NU % 2][:, o + k:o + k + 1])
                ins.then_inc(s["tt"], 1)

            def carry(n):
                cy = CY[n % 2][(n // 2 + 1) % 2]
                e.wait_ge(s["ch"], carries(n) + 1)
                e.tensor_tensor(cy[:, 1, :], banks[6 + n % 2][:, 0:NBIN], cy[:, 0, :], ALU.subtract).then_inc(s["cy"], 1)

            def places(i):
                k = i % 2
                e.wait_ge(s["tt"], NU * (i + 1))
                link(e.tensor_copy(PI[:, :], POS[k][:, :]))
                e.tensor_scalar(i1[:, :], PI[:, :], LR, P - 1, ALU.arith_shift_right, ALU.bitwise_and)
                e.tensor_scalar(i2[:, :], PI[:, :], 7 + LR, LR, ALU.arith_shift_right, ALU.logical_shift_left)
                link(e.tensor_single_scalar(i3[:, :], PI[:, :], R - 1, op=ALU.bitwise_and))
                e.tensor_copy(AF[k][:, :], i1[:, :])
                e.tensor_scalar(AFn[k][:, :], i1[:, :], -1.0, None, ALU.mult)
                e.tensor_tensor(BF[k][:, :], i2[:, :], i3[:, :], ALU.add).then_inc(s["ps"], 1)

            def colhot(m):
                k, o = m // (NU // 2) % 2, m % (NU // 2) * 8
                e.wait_ge(s["ps"], m // (NU // 2) + 1)
                link_m[m] = mark(e.tensor_tensor(
                    OHB[m % 2], iof[:, 0:CW].rearrange("p (a w) -> p a w", a=1).broadcast_to([P, 8, CW]),
                    BF[k][:, o:o + 8].rearrange("p (c w) -> p c w", w=1).broadcast_to([P, 8, CW]), ALU.is_equal))

            def colval(m):
                e.wait_ge(s_v, link_m[m])
                e.wait_ge(s["vw"], 1)
                ge(e, s["so"], 2 * (m - 1))
                c = 8 * m
                e.tensor_tensor(BV[m % 2], OHB[m % 2].rearrange("p c (v b) -> p c v b", v=1).broadcast_to([P, 8, 2, CW]),
                                VAL[:, c:c + 8, :].rearrange("p c (v b) -> p c v b", b=1).broadcast_to([P, 8, 2, CW]),
                                ALU.mult).then_inc(s["bv"], 1)

            def rowhot(v):
                e.wait_ge(s["ps"], v // NU + 1)
                ge(e, s["so"], v - 3)
                o = v % NU * GC
                e.tensor_scalar(AO[v % 4][:, 0, :], iof[:, :], AF[v // NU % 2][:, o:o + 1], None, ALU.is_equal)\
                 .then_inc(s["a0"], 1)

            def records(q):
                k = q % 4
                if q >= 4:
                    e.wait_ge(s[f"scat{k}"], 16 * CHB * (q // 4))
                rec = REC[k].rearrange("p (b w) -> p b w", w=4)
                z = banks[2 + q % 2]
                e.wait_ge(s["so"], 8 * (q + 1))
                m1 = mark(e.tensor_copy(pki[:, :], z[:, 0:CW]))
                e.wait_ge(s["dd"], q + 1)
                m0 = mark(e.tensor_reduce(dsum[:, :], banks[4][:, 0:3 * CHB].rearrange("p (m k) -> p m k", k=3),
                                          axis=AX.X, op=ALU.add))
                e.tensor_copy(rec[:, :, 2:3].bitcast(fp32), z[:, CW:2 * CW].rearrange("p (b w) -> p b w", w=1))\
                 .then_inc(s["up"], 1)
                e.wait_ge(s_v, m1)
                m2 = mark(e.tensor_single_scalar(shi[:, :], pki[:, :], 14, op=ALU.arith_shift_right))
                e.tensor_single_scalar(rec[:, :, 1:2], pki[:, :].rearrange("p (b w) -> p b w", w=1), 16383,
                                       op=ALU.bitwise_and)
                e.wait_ge(s_v, m0)
                e.scalar_tensor_tensor(out=IDX[k][:, :], in0=dsum[:, :], scalar=0.5, in1=DCI[:, q, :],
                                       op0=ALU.mult, op1=ALU.add).then_inc(s["dr"], 1)
                e.wait_ge(s_v, m2)
                e.tensor_scalar(rec[:, :, 0:1].bitcast(fp32), shi[:, :].rearrange("p (b w) -> p b w", w=1), -1.0,
                                None, ALU.add).then_inc(s["rec"], 1)

            def tile_blocks(k, half):
                if half == 0:
                    if k:
                        link(e.tensor_scalar(cl[:, 6:7], cl[:, 6:7], -float(NG), None, ALU.add))
                    e.tensor_scalar(MT[0:NB, :, :].rearrange("p a b -> p (a b)")[:, 0:NG], IOT[0:NB, :],
                                    cl[0:NB, 6:7], None, ALU.is_ge).then_inc(s["m"], 1)
                else:
                    e.wait_ge(s["mb"], k + 1)
                    link(e.tensor_scalar(BT[0:1, k * NG:(k + 1) * NG], banks[4][0:1, 0:NG],
                                         float(NB - 1), float(HF), ALU.min, ALU.mult))

            def bc(t):
                return t.rearrange("p (b f) -> p b f", f=1).broadcast_to([P, CB, NF])

            def norm1(q, _):
                X = XC[q % 2]
                nx = sum(16 * (1 + (r == NCH - 1)) for r in range(q % 2, q + 1, 2))
                e.wait_ge(s_x[q % 2], nx)
                link(e.tensor_reduce(st[:, 0, :], X[:, :, :], axis=AX.X, op=ALU.add))
                link(e.tensor_scalar(st[:, 1, :], st[:, 0, :], 1.0 / NF, None, ALU.mult))
                link(e.tensor_tensor(XM[:, :, :], X[:, :, :], bc(st[:, 1, :]), ALU.subtract))
                e.sem_inc(s["xm"], 1)
                if q == NCH - 3:
                    e.memset(X[:, CB - 1, :], 0.0).then_inc(s["ms"], 1)
                link(e.tensor_tensor(SQ[:, :, :], XM[:, :, :], XM[:, :, :], ALU.mult))
                link(e.tensor_reduce(st[:, 2, :], SQ[:, :, :], axis=AX.X, op=ALU.add))
                e.tensor_scalar(st[:, 2, :], st[:, 2, :], 1.0 / NF, EPS, ALU.mult, ALU.add).then_inc(s["var"], 1)

            def norm2(q, _):
                e.wait_ge(s["rt"], q + 1)
                link(e.reciprocal(st[:, 3, :], st[:, 3, :]))
                link(e.tensor_tensor(XM[:, :, :], XM[:, :, :], bc(st[:, 3, :]), ALU.mult))
                ge(e, s["t1"], q - 1)
                e.tensor_scalar(H[q % 2][:, :, :], XM[:, :, :], 0.0, None, ALU.max).then_inc(s["h"], 1)

            def rest1(q, b):
                B = q * CB + b
                e.wait_ge(s["qc"], B + 1)
                o = HF * B
                e.tensor_tensor(RS[B % 2][:, :], banks[5][:, 0:HF], P3[0][:, o:o + HF],
                                ALU.subtract).then_inc(s["r1"], 1)

            def rest2(q, b):
                B = q * CB + b
                o = HF * B
                e.wait_ge(s["p2c"], B + 1)
                e.tensor_tensor(P3[2][:, o:o + HF], RS[B % 2][:, :],
                                P3[1][:, o:o + HF], ALU.subtract).then_inc(s["p3"], 1)

            node = node_steps(((0, 0, norm1), (0, 4, norm2), (2, None, rest1), (4, None, rest2)))
            link_m = {}
            onehot(0)
            onehot(1)
            link(e.tensor_scalar(T32, SRC, P - 1, 14, ALU.bitwise_and, ALU.logical_shift_left))
            link(e.tensor_tensor(T32, T32, DST, ALU.add))
            link(e.tensor_scalar(VAL[:, :, 0:1], T32.rearrange("p (c w) -> p c w", w=1), 16384.0, None, ALU.add))
            for t in range(NR + OFF + 3):
                v = t - OFF
                if t + 2 < NR:
                    onehot(t + 2)
                if t < NR and t % NU < NU - 2:
                    carry(t)
                if t < NR:
                    ranks(t)
                if t % NU == NU - 1 and t < NR:
                    places(t // NU)
                if 0 <= v < NR and v % 2 == 0:
                    rowhot(v)
                if 0 <= v < NR and v % 2 == 0:
                    colval(v // 2)
                if v >= -1 and v % 2 == 1 and v + 1 < NR:
                    colhot((v + 1) // 2)
                if v >= 8 and v % 8 == 2:
                    records(v // 8 - 1)
                if 2 <= t < 14:
                    if (t - 2) % 3 < 2:
                        tile_blocks((t - 2) // 3, (t - 2) % 3)
                for f, q, b in node.get(t, ()):
                    f(q, b)
            e.wait_ge(s["w"], 16 * 11)
            cur = b2_bc
            for q in range(3):
                e.tensor_scalar(msk[:, q:q + 1], pidx[:, :], float(q), None, ALU.is_equal)
                link(e.tensor_copy(b2s[:, q, :], cur[:, :]))
                if q < 2:
                    link(e.tensor_tensor(b2r[:, :], cur[:, :], b2s[:, q, :], ALU.subtract))
                    cur = b2r
            for q in range(3):
                link(e.tensor_scalar(b2s[:, q, :], b2s[:, q, :], msk[:, q:q + 1], None, ALU.mult))
            link(e.tensor_tensor(b2s[:, 0, :], b2s[:, 0, :], b2s[:, 1, :], ALU.add))
            link(e.tensor_tensor(b2s[:, 0, :], b2s[:, 0, :], b2s[:, 2, :], ALU.add))
            link(e.tensor_copy(B2[:, :, :], b2s[:, 0:1, :].broadcast_to([P, U, HF])))
            link(e.memset(AGG[:, 0:OREC], 0.0))
            for k in range(4):
                e.wait_ge(s[f"scat{k}"], 16 * CHB * (NS // 4))
            e.memset(AGG[:, OREC:NPAD], 0.0).then_inc(s["ad"], 1)

            def build(g, k, n):
                e.wait_ge(s_rec[k], n * 16 + 16)
                ge(e, s["tp"], g - 3)
                ge(e, s["of"], g - 3)
                for u in range(U):
                    ins = e.tensor_scalar(OHb[k][:, u, :], iob[:, :], RB[k][:, u, 0:1].bitcast(fp32),
                                          None, ALU.is_equal)
                ins.then_inc(s["oh"], 1)

            def weigh(i, k):
                for u in range(U):
                    e.wait_ge(s_g[k * U + u], i * 16 + 16)
                    ins = e.scalar_tensor_tensor(out=G[k * U + u], in0=c_bc[:, :],
                                                 scalar=RB[k][:, u, 2:3].bitcast(fp32),
                                                 in1=G[k * U + u], op0=ALU.mult, op1=ALU.add)
                ins.then_inc(s["st"], 1)

            def add(g, k):
                e.wait_ge(s["ap"], g + 1)
                vs = blocks(g, mybir.EngineType.DVE)
                for u, v in enumerate(vs):
                    e.wait_ge(s["ad"], g * U + (u + 1))
                    e.tensor_tensor(AGG[:, ds(v, P)], banks[6 + k % 2][:, u * P:(u + 1) * P],
                                    AGG[:, ds(v, P)], ALU.add).then_inc(s["ad"], 1)

            build(0, 0, 0)
            for k in range(4):
                build(k + 1, (k + 1) % 4, (k + 1) // 4)
                weigh(0, k)
                if k >= 2:
                    add(k - 2, k - 2)
            with e.Fori(1, NG // 4 - 1) as i:
                for k in range(4):
                    build(i * 4 + (k + 1), (k + 1) % 4, i + (k + 1) // 4)
                    weigh(i, k)
                    add(i * 4 + (k - 2), k % 4)
            for g in range(4 * (NG // 4 - 1), NG):
                if g + 1 < NG:
                    build(g + 1, (g + 1) % 4, (g + 1) // 4)
                weigh(g // 4, g % 4)
                add(g - 2, (g - 2) % 4)
            for g in (NG - 2, NG - 1):
                add(g, g % 4)
            def bias(q):
                a, b = q * QB, min(NB, (q + 1) * QB)
                e.wait_ge(s_fx[q], 32 + 16 * (b == NB))
                for lo, hi, rows in ((a, min(b, NB - 1), P), (NB - 1, b, LAST)):
                    if lo < hi:
                        nbb = nb2_bc[0:rows, :].rearrange("p (a f) -> p a f", a=1).broadcast_to([rows, hi - lo, NF])
                        e.tensor_tensor(XA[0:rows, lo:hi, :], XA[0:rows, lo:hi, :], nbb, ALU.add).then_inc(s["fb"], 1)

            for q in range(NQ):
                bias(q)
            for q, nb in enumerate(nchunk):
                e.wait_ge(s["fu"], q + 1)
                a = 4 * q
                e.wait_ge(s["fb"], min(NQ, (a + nb - 1) // QB + 1) + (a + nb == NB))
                z = banks[4 + q % 4][:, 0:nb * NF].rearrange("p (b f) -> p b f", f=NF)
                full_b = nb - (a + nb == NB)
                if full_b:
                    ins = e.tensor_tensor(XA[:, a:a + full_b, :], z[:, 0:full_b, :], XA[:, a:a + full_b, :], ALU.add)
                if full_b < nb:
                    ins = e.tensor_tensor(XA[0:LAST, NB - 1, :], z[0:LAST, full_b, :], XA[0:LAST, NB - 1, :], ALU.add)
                ins.then_inc(s["fo"], 1)

        @block.tensor
        def _(e):
            e.wait_ge(s["io"], 5)
            def total(r):
                e.wait_ge(s["rr"], r + 1)
                for k in range(4):
                    e.matmul(banks[2][:, 4 * r + k:4 * r + k + 1], HM[r % 2][:, k * P:(k + 1) * P], onesf[0:32, 0:1],
                             start=True, stop=True).then_inc(s["hc"], 1)

            for q in range(NS):
                g, h = q // 2, q % 2
                e.wait_ge(s["o1"], g + 1)
                if q % 4 == 0:
                    ge(e, s["rr"], q // 4 - 1)
                for m in range(8):
                    c = SC * h + m * 4
                    last = e.matmul(banks[q // 4 % 2][0:32, q % 4 * 64:q % 4 * 64 + 64],
                                    OA[g % 2][:, c:c + 4, :].rearrange("p c h -> p (c h)"),
                                    OB[g % 2][:, c:c + 4, :].rearrange("p c l -> p (c l)"),
                                    start=(m == 0), stop=(m == 7))
                if h:
                    last.then_inc(s["f1"], 1)
                if q % 4 == 3 and q > 4:
                    total(q // 4 - 1)
            total(NS // 4 - 1)
            e.wait_ge(s["cc"], 1)
            e.matmul(banks[3][:, 0:NS], Lf[:, :], ccT[:, :], start=True, stop=True).then_inc(s["lb"], 1)
            e.wait_ge(s["tl"], 1)
            e.matmul(banks[4][:, 0:1], Lf[:, :], cl[:, 4:5], start=True, stop=True).then_inc(s["tb"], 1)
            e.wait_ge(s["df"], 1)
            e.matmul(banks[3][:, 0:NS], DM[:, :], dl[:, :], start=True, stop=True).then_inc(s["df"], 1)

            def base(n):
                if unit(n)[1] == 0:
                    e.wait_ge(s["lbb"], n // NU * 2 + n % 2 + 1)
                    return [(LB[n % 2], identf[:, 0:NBIN])]
                e.wait_ge(s["cy"], carries(n - 2) + 1)
                return [(identb, CY[n % 2][n // 2 % 2][:, h, :]) for h in range(2)]

            def carry(n):
                parts = base(n)
                oh = OH[n % 2][n // 2 % 4][:, :, :].rearrange("p a b -> p (a b)")
                if n >= NU and unit(n)[1] == 0:
                    e.wait_ge(s["cy"], carries(n - 4) + 1)
                e.wait_ge(s["o2"], n + 1)
                for h, (w, c) in enumerate(parts):
                    e.matmul(banks[6 + n % 2][:, 0:NBIN], w[:, :], c, start=(h == 0), stop=False)
                for k in range(GC):
                    last = e.matmul(banks[6 + n % 2][:, 0:NBIN], ones[:, :], oh[:, k * NBIN:(k + 1) * NBIN],
                                    start=False, stop=(k == GC - 1))
                last.then_inc(s["cr"], 1)

            def ladder(n):
                z = banks[n % 2]
                oh = OH[n % 2][n // 2 % 4][:, :, :].rearrange("p a b -> p (a b)")
                parts = base(n)
                e.wait_ge(s["o2"], n + 1)
                ge(e, s["tt"], n - 1)
                for h, (w, c) in enumerate(parts):
                    e.matmul(z[:, 0:WC].rearrange("p (c b) -> p c b", b=NBIN), w[:, :],
                             c.rearrange("p (a b) -> p a b", a=1).broadcast_to([P, GC, NBIN]),
                             start=(h == 0), stop=False)
                e.matmul(z[:, 0:WC], Lm[:, :], oh, start=False, stop=False)
                for k in range(1, GC):
                    last = e.matmul(z[:, k * NBIN:WC], ones[:, :], oh[:, 0:WC - k * NBIN],
                                    start=False, stop=(k == GC - 1))
                last.then_inc(s["p2"], 1)

            def place(v):
                q = v // 8
                if v % 8 == 0:
                    ge(e, s["up"], q - 1)
                e.wait_ge(s["bv"], v // 2 + 1)
                e.wait_ge(s["a0"], v // 2 + 1)
                e.wait_ge(s["a1"], v + 1)
                for k in range(GC):
                    last = e.matmul(banks[2 + q % 2][:, 0:2 * CW], AO[v % 4][:, k, :],
                                    BV[v // 2 % 2][:, v % 2 * GC + k, :, :].rearrange("p v b -> p (v b)"),
                                    start=(v % 8 == 0 and k == 0), stop=(v % 8 == 7 and k == GC - 1))
                last.then_inc(s["so"], 1)

            def chunks(q):
                e.wait_ge(s["mm"], 2 * q + 2)
                ge(e, s["dr"], q)
                for m in range(CHB):
                    last = e.matmul(banks[4][:, 3 * m:3 * m + 3], MM[0:NBIN, m * P:(m + 1) * P], dd3[0:NBIN, q, :],
                                    start=True, stop=True)
                last.then_inc(s["dd"], 1)

            def flip(q, hb):
                if hb == 0:
                    e.wait_ge(s["w"], 16 * 11)
                    e.wait_ge(s["h"], q + 1)
                    ge(e, s["r1"], CB * q)
                    ge(e, s["qc"], CB * q)
                else:
                    e.wait_ge(s["ht"], 2 * q + 1)
                for b in range(4 * hb, min(CB, 4 * hb + 4)):
                    last = e.matmul(banks[5][0:NF, (b - 4 * hb) * P:(b - 4 * hb + 1) * P],
                                    H[q % 2][:, b, :], identf[:, :], start=True, stop=True)
                last.then_inc(s["t1"] if hb else s["hd"], 1)

            def pq(q, b):
                B = q * CB + b
                e.wait_ge(s["ht"], 2 * (q + 1))
                ge(e, s["r1"], B)
                ge(e, s["qc"], B)
                e.matmul(banks[5][:, 0:2 * HF], HT[q % 2][:, b * P:(b + 1) * P],
                         W1ab[:, :, :].rearrange("p a b -> p (a b)"), start=True, stop=True).then_inc(s["pq"], 1)

            node = node_steps(((0, 6, lambda q, _: flip(q, 0)), (0, 8, lambda q, _: flip(q, 1)), (0, None, pq)))
            for t in range(NR + OFF + 3):
                v = t - OFF
                for n in ((0, 1) if t == 0 else (t + 1,)):
                    if n < NR and n % NU < NU - 2:
                        carry(n)
                if t < NR:
                    ladder(t)
                if 0 <= v - 2 < NR:
                    place(v - 2)
                if 0 <= v < NR and v % 8 == 4:
                    chunks(v // 8)
                if 2 <= t < 14 and (t - 2) % 3 == 0:
                    k = (t - 2) // 3
                    e.wait_ge(s["m"], k + 1)
                    e.matmul(banks[4][0:1, 0:NG], ones[0:NB, 0:1],
                             MT[0:NB, :, :].rearrange("p a b -> p (a b)")[:, 0:NG],
                             start=True, stop=True).then_inc(s["mb"], 1)
                for f, q, b in node.get(t, ()):
                    f(q, b)

            def mA(g, k):
                e.wait_ge(s["oh"], g + 1)
                ge(e, s["oT"], g - 1)
                tp = TPb[k % 2]
                for u in range(U):
                    last = e.transpose(tp[:, u * P:(u + 1) * P], OHb[k][:, u, :], identb[:, :])
                last.then_inc(s["tp"], 1)

            def mB(g, k):
                vs = blocks(g, mybir.EngineType.PE)
                e.wait_ge(s["oT"], g + 1)
                e.wait_ge(s["st"], g + 1)
                ge(e, s["e1"], g - 1)
                for u, v in enumerate(vs):
                    z = banks[2 + k % 2][:, u * P:(u + 1) * P]
                    e.matmul(z, G[k * U + u], identf[:, :], start=True, stop=False)
                    for q in range(3):
                        last = e.matmul(z, P3[q][:, ds(v, HF)], OHT[k % 2][:, u * P:(u + 1) * P],
                                        start=False, stop=(q == 2))
                last.then_inc(s["z1"], 1)

            def mC(g, k):
                e.wait_ge(s["e1"], g + 1)
                ge(e, s["e2"], g - 1)
                z = banks[4 + k % 2]
                e.matmul(z[:, :], ones[:, :], B2[:, :, :].rearrange("p a b -> p (a b)"), start=True, stop=False)
                for u in range(U):
                    last = e.matmul(z[:, u * HF:(u + 1) * HF], E1[k % 2][:, u * P:(u + 1) * P], W2[:, :],
                                    start=False, stop=(u == U - 1))
                last.then_inc(s["z2"], 1)

            def mD(g, k):
                e.wait_ge(s["e2"], g + 1)
                e.wait_ge(s["of"], g + 1)
                ge(e, s["ad"], (g - 1) * U + 1)
                for u in range(U):
                    last = e.matmul(banks[6 + k % 2][:, u * P:(u + 1) * P], E2[k % 2][:, u * HF:(u + 1) * HF],
                                    OHf[k][:, u, :], start=True, stop=True)
                last.then_inc(s["ap"], 1)

            e.wait_ge(s["p3"], NB)
            e.wait_ge(s["qc"], NB)
            for k in range(4):
                mA(k, k)
                if k >= 2:
                    mD(k - 2, k - 2)
                if k >= 1:
                    mC(k - 1, k - 1)
                mB(k, k)
            with e.Fori(1, NG // 4) as i:
                for k in range(4):
                    g = i * 4 + k
                    mA(g, k)
                    mD(i * 4 + (k - 2), (k - 2) % 4)
                    mC(i * 4 + (k - 1), (k - 1) % 4)
                    mB(g, k)
            for g in range(4 * (NG // 4), NG):
                mA(g, g % 4)
                mD(g - 2, (g - 2) % 4)
                mC(g - 1, (g - 1) % 4)
                mB(g, g % 4)
            mD(NG - 2, (NG - 2) % 4)
            mC(NG - 1, (NG - 1) % 4)
            mD(NG - 1, (NG - 1) % 4)
            e.wait_ge(s["ad"], NT + 1)
            def inner(q):
                nb = nchunk[q]
                a = 4 * q
                for r0 in range(a // QB, (a + nb - 1) // QB + 1):
                    e.wait_ge(s_fx[r0], 32 + 16 * (r0 == NQ - 1))
                ge(e, s["fd"], q - 3)
                z = banks[q % 4][:, 0:nb * P]
                e.matmul(z, nW1b[:, :], AGG[:, q * 512:q * 512 + nb * P], start=True, stop=False)
                e.matmul(z, nW1a[:, :], HA[:, q * 512:q * 512 + nb * P], start=False, stop=True).then_inc(s["fz"], 1)

            def outer(r):
                e.wait_ge(s["fd"], r + 1)
                ge(e, s["fo"], r - 3)
                for b in range(nchunk[r]):
                    last = e.matmul(banks[4 + r % 4][:, b * NF:(b + 1) * NF], F1[r % 4][:, b * P:(b + 1) * P],
                                    nW2s[:, :], start=True, stop=True)
                last.then_inc(s["fu"], 1)

            nq = len(nchunk)
            for q in range(0, nq + 2, 2):
                for r in range(q, min(q + 2, nq)):
                    inner(r)
                for r in range(max(q - 2, 0), min(q, nq)):
                    outer(r)

        @block.scalar
        def _(e):
            e.wait_ge(s["ms"], 3)
            ewf = ew.rearrange("n a -> (n a)")
            e.dma_start(TWv[0:P - 1, :], ewf[0:full].rearrange("(p c) -> p c", c=C)).then_inc(s["edc"], 16)
            e.dma_start(TWv[P - 1:P, 0:LASTC], ewf[full:E].rearrange("(p c) -> p c", c=LASTC)).then_inc(s["edc"], 16)
            def base(i):
                e.wait_ge(s["dq"], 1)
                for j in range(2):
                    ge(e, s["p2"], NU * (i - 1) + j + 1)
                    e.activation(LB[j][:, :], onesf[:, :], ACT.Copy, scale=lbR[:, 2 * i + j:2 * i + j + 1])\
                     .then_inc(s["lbb"], 1)

            def carry(n):
                e.wait_ge(s["cr"], carries(n) + 1)
                e.activation(CY[n % 2][(n // 2 + 1) % 2][:, 0, :], banks[6 + n % 2][:, 0:NBIN], ACT.Copy).then_inc(s["ch"], 1)

            def away(v):
                e.wait_ge(s["ps"], v // NU + 1)
                ge(e, s["a1"], v - 1)
                o = v % NU * GC
                for k in range(v % 2 == 0, GC):
                    ins = e.activation(AB[v % 2][:, k, :], iof[:, :], ACT.Abs,
                                       bias=AFn[v // NU % 2][:, o + k:o + k + 1])
                ins.then_inc(s["ab"], 1)

            def rowhot(v):
                e.wait_ge(s["ab"], v + 1)
                ge(e, s["so"], v - 3)
                k = int(v % 2 == 0)
                e.activation(AO[v % 4][:, k:GC, :], AB[v % 2][:, k:GC, :], ACT.Relu, scale=-1.0, bias=onesf[:, 0:1])\
                 .then_inc(s["a1"], 1)

            def chunksign(q, h):
                if h == 0:
                    ge(e, s["dd"], q)
                c = slice(h * (CHB // 2) * P, (CHB // 2) * P if h == 0 else CH)
                e.activation(MM[0:NBIN, c], IOJ[0:NBIN, c], ACT.Sign, bias=lbn[0:NBIN, q:q + 1]).then_inc(s["mm"], 1)

            def root(q, _):
                e.wait_ge(s["var"], q + 1)
                e.activation(st[:, 3, :], st[:, 2, :], ACT.Sqrt).then_inc(s["rt"], 1)

            def tohT(q, hb):
                if hb == 0 and q >= 2:
                    e.wait_ge(s_hq[q % 2], 32 * (q // 2))
                e.wait_ge(s["t1"] if hb else s["hd"], q + 1)
                n = (4 - hb) * P
                if hb == 0:
                    n = 4 * P
                e.activation(HT[q % 2][:, hb * 512:hb * 512 + n], banks[5][0:NF, 0:n], ACT.Copy).then_inc(s["ht"], 1)

            def split1(q, b):
                B = q * CB + b
                o = HF * B
                e.wait_ge(s["pq"], B + 1)
                z = banks[5]
                e.activation(P3[0][:, o:o + HF], z[:, 0:HF], ACT.Copy)
                e.activation(QS[q % 2][:, b, :], z[:, HF:2 * HF], ACT.Copy).then_inc(s["qc"], 1)

            def split2(q, b):
                B = q * CB + b
                o = HF * B
                e.wait_ge(s["r1"], B + 1)
                e.activation(P3[1][:, o:o + HF], RS[B % 2][:, :], ACT.Copy).then_inc(s["p2c"], 1)

            node = node_steps(((0, 2, root), (0, 7, lambda q, _: tohT(q, 0)), (0, 9, lambda q, _: tohT(q, 1)),
                               (1, None, split1), (3, None, split2)))
            e.wait_ge(s["edc"], 32)
            e.activation(VAL[:, :, 1:2], TWv.rearrange("p (c w) -> p c w", w=1), ACT.Copy).then_inc(s["vw"], 1)
            base(0)
            for t in range(NR + OFF + 3):
                v = t - OFF
                if t % NU == NU - 4 and t < NR - NU:
                    base(t // NU + 1)
                if 0 <= v < NR:
                    away(v)
                if 0 <= v - 1 < NR:
                    rowhot(v - 1)
                for n in ((0, 1) if t == 0 else (t + 1,)):
                    if n < NR and n % NU < NU - 2:
                        carry(n)
                if 0 <= v < NR and v % 8 in (1, 2):
                    chunksign(v // 8, v % 8 - 1)
                for f, q, b in node.get(t, ()):
                    f(q, b)

            def tcopy(g, k):
                e.wait_ge(s["tp"], g + 1)
                ge(e, s["z1"], g - 1)
                e.activation(OHT[k % 2][:, :], TPb[k % 2], ACT.Copy).then_inc(s["oT"], 1)
                ge(e, s["ap"], g - 3)
                e.activation(OHf[k], OHb[k][:, :, :], ACT.Copy).then_inc(s["of"], 1)

            def silu1(g, k):
                e.wait_ge(s["z1"], g + 1)
                ge(e, s["z2"], g - 1)
                e.activation(E1[k % 2], banks[2 + k % 2][:, :], ACT.Silu, bias=eb1c[:, :]).then_inc(s["e1"], 1)

            def silu2(g, k):
                e.wait_ge(s["z2"], g + 1)
                ge(e, s["ap"], g - 1)
                e.activation(E2[k % 2], banks[4 + k % 2][:, :], ACT.Silu).then_inc(s["e2"], 1)

            e.wait_ge(s["w"], 16 * 11)
            for k in range(4):
                tcopy(k, k)
                if k:
                    silu2(k - 1, k - 1)
                silu1(k, k)
            with e.Fori(1, NG // 4) as i:
                for k in range(4):
                    g = i * 4 + k
                    tcopy(g, k)
                    silu2(i * 4 + (k - 1), (k - 1) % 4)
                    silu1(g, k)
            for g in range(4 * (NG // 4), NG):
                tcopy(g, g % 4)
                silu2(g - 1, (g - 1) % 4)
                silu1(g, g % 4)
            silu2(NG - 1, (NG - 1) % 4)
            for q, nb in enumerate(nchunk):
                e.wait_ge(s["fz"], q + 1)
                ge(e, s["fu"], q - 3)
                e.activation(F1[q % 4][:, 0:nb * P], banks[q % 4][:, 0:nb * P], ACT.Silu, bias=nb1c[:, :])\
                 .then_inc(s["fd"], 1)


_INS = ["x", "src", "dst", "edge_weight1", "L0_gnn_eW1", "L0_gnn_eb1", "L0_gnn_eW2", "L0_gnn_eb2",
        "L0_gnn_nW1", "L0_gnn_nb1", "L0_gnn_nW2", "L0_gnn_nb2"]


def kernel(**inputs):
    import numpy as _np
    import concourse.bacc as _bacc
    from concourse import mybir as _mybir
    from concourse.bass_utils import run_bass_kernel_spmd as _run

    nc = _bacc.Bacc("TRN2", target_bir_lowering=False, num_devices=1)
    arrays, args = {}, []
    for name in _INS:
        a = _np.ascontiguousarray(inputs[name])
        arrays[f"in_{name}"] = a
        args.append(nc.dram_tensor(f"in_{name}", a.shape, _mybir.dt.from_np(a.dtype), kind="ExternalInput").ap())
    out = nc.dram_tensor("out_0", (N, NF), _mybir.dt.float32, kind="ExternalOutput").ap()
    gnn(nc, *args, out)
    return _run(nc, [arrays], core_ids=[0]).results[0]["out_0"]
```
